# Optimizing a Trainium2 kernel written in Bass

```python
import numpy as np
import jax
import jax.numpy as jnp

def _softmax(x, axis=-1):
    return jax.nn.softmax(x, axis=axis)

def _gelu(x):
    return jax.nn.gelu(x, approximate=True)

def _silu(x):
    return jax.nn.silu(x)

def _sigmoid(x):
    return jax.nn.sigmoid(x)

def _layernorm(x, axis=-1, eps=1e-05):
    m = jnp.mean(x, axis=axis, keepdims=True)
    v = jnp.var(x, axis=axis, keepdims=True)
    return (x - m) / jnp.sqrt(v + eps)

def _scatter_add(tgt, idx, src, axis=0):
    return tgt.at[idx].add(src)

def _segment_sum(src, seg, n):
    return jax.ops.segment_sum(src, seg, n)
kernel_name = 'mk_dlrm_tower_d1_rec_r8_7ca2cd'

def setup_inputs(seed: int=0):
    np.random.seed(seed)
    _w = jnp.asarray

    def _rec_inputs():
        import jax
        import jax.numpy as jnp
        _tk = jax.random.key(seed)
        dense_ctx = jax.random.normal(jax.random.fold_in(_tk, 190), (512, 16), jnp.float32)
        ids = jnp.stack([jax.random.randint(jax.random.fold_in(_tk, 200 + f), (512,), 0, v, jnp.int32) for f, v in enumerate([1000, 1000, 1000, 1000, 125000, 1250, 1000, 1000, 1250, 1250, 1000, 12500, 12500, 125000, 1000, 1000, 12500, 12500, 1000, 1000, 125000, 12500, 1250, 125000])], axis=1)
        tbl_0 = 0.05 * jax.random.normal(jax.random.fold_in(_tk, 500 + 0), (1000, 16), jnp.float32)
        tbl_1 = 0.05 * jax.random.normal(jax.random.fold_in(_tk, 500 + 1), (1000, 16), jnp.float32)
        tbl_2 = 0.05 * jax.random.normal(jax.random.fold_in(_tk, 500 + 2), (1000, 16), jnp.float32)
        tbl_3 = 0.05 * jax.random.normal(jax.random.fold_in(_tk, 500 + 3), (1000, 16), jnp.float32)
        tbl_4 = 0.05 * jax.random.normal(jax.random.fold_in(_tk, 500 + 4), (125000, 16), jnp.float32)
        tbl_5 = 0.05 * jax.random.normal(jax.random.fold_in(_tk, 500 + 5), (1250, 16), jnp.float32)
        tbl_6 = 0.05 * jax.random.normal(jax.random.fold_in(_tk, 500 + 6), (1000, 16), jnp.float32)
        tbl_7 = 0.05 * jax.random.normal(jax.random.fold_in(_tk, 500 + 7), (1000, 16), jnp.float32)
        tbl_8 = 0.05 * jax.random.normal(jax.random.fold_in(_tk, 500 + 8), (1250, 16), jnp.float32)
        tbl_9 = 0.05 * jax.random.normal(jax.random.fold_in(_tk, 500 + 9), (1250, 16), jnp.float32)
        tbl_10 = 0.05 * jax.random.normal(jax.random.fold_in(_tk, 500 + 10), (1000, 16), jnp.float32)
        tbl_11 = 0.05 * jax.random.normal(jax.random.fold_in(_tk, 500 + 11), (12500, 16), jnp.float32)
        tbl_12 = 0.05 * jax.random.normal(jax.random.fold_in(_tk, 500 + 12), (12500, 16), jnp.float32)
        tbl_13 = 0.05 * jax.random.normal(jax.random.fold_in(_tk, 500 + 13), (125000, 16), jnp.float32)
        tbl_14 = 0.05 * jax.random.normal(jax.random.fold_in(_tk, 500 + 14), (1000, 16), jnp.float32)
        tbl_15 = 0.05 * jax.random.normal(jax.random.fold_in(_tk, 500 + 15), (1000, 16), jnp.float32)
        tbl_16 = 0.05 * jax.random.normal(jax.random.fold_in(_tk, 500 + 16), (12500, 16), jnp.float32)
        tbl_17 = 0.05 * jax.random.normal(jax.random.fold_in(_tk, 500 + 17), (12500, 16), jnp.float32)
        tbl_18 = 0.05 * jax.random.normal(jax.random.fold_in(_tk, 500 + 18), (1000, 16), jnp.float32)
        tbl_19 = 0.05 * jax.random.normal(jax.random.fold_in(_tk, 500 + 19), (1000, 16), jnp.float32)
        tbl_20 = 0.05 * jax.random.normal(jax.random.fold_in(_tk, 500 + 20), (125000, 16), jnp.float32)
        tbl_21 = 0.05 * jax.random.normal(jax.random.fold_in(_tk, 500 + 21), (12500, 16), jnp.float32)
        tbl_22 = 0.05 * jax.random.normal(jax.random.fold_in(_tk, 500 + 22), (1250, 16), jnp.float32)
        tbl_23 = 0.05 * jax.random.normal(jax.random.fold_in(_tk, 500 + 23), (125000, 16), jnp.float32)
        _rk = jax.random.fold_in(_tk, 7)
        W_top1 = 0.0693375 * jax.random.normal(jax.random.fold_in(_tk, 801), (208, 512), jnp.float32)
        W_top2 = 0.0441942 * jax.random.normal(jax.random.fold_in(_tk, 802), (512, 256), jnp.float32)
        W_top3 = 0.0625 * jax.random.normal(jax.random.fold_in(_tk, 803), (256, 1), jnp.float32)
        b_top1 = jnp.zeros((512,), jnp.float32)
        b_top2 = jnp.zeros((256,), jnp.float32)
        return (dense_ctx, ids, tbl_0, tbl_1, tbl_2, tbl_3, tbl_4, tbl_5, tbl_6, tbl_7, tbl_8, tbl_9, tbl_10, tbl_11, tbl_12, tbl_13, tbl_14, tbl_15, tbl_16, tbl_17, tbl_18, tbl_19, tbl_20, tbl_21, tbl_22, tbl_23, W_top1, b_top1, W_top2, b_top2, W_top3)
    dense_ctx, ids, tbl_0, tbl_1, tbl_2, tbl_3, tbl_4, tbl_5, tbl_6, tbl_7, tbl_8, tbl_9, tbl_10, tbl_11, tbl_12, tbl_13, tbl_14, tbl_15, tbl_16, tbl_17, tbl_18, tbl_19, tbl_20, tbl_21, tbl_22, tbl_23, W_top1, b_top1, W_top2, b_top2, W_top3 = _rec_inputs()

    def _L0_rec_setup():
        import jax, jax.numpy as jnp
        import numpy as np
        B, F, D = (512, 24, 16)
        LAYER_SIZES = [64, 64, 64]

        def _cin_forward(X0, Ws):
            F_ = X0.shape[1]
            Xk = X0
            outs = []
            for W in Ws:
                H_prev = Xk.shape[1]
                Wr = W.reshape(F_, H_prev, W.shape[1])
                Xk = jnp.einsum('bfd,bhd,fho->bod', X0, Xk, Wr)
                outs.append(Xk.sum(axis=2))
            return jnp.concatenate(outs, axis=1)
        key = jax.random.key(seed)
        k0, k1, k2, k3 = jax.random.split(key, 4)
        X0 = jax.random.normal(k0, (B, F, D), dtype=jnp.float32)
        prev = F
        Ws = []
        for k, h in zip((k1, k2, k3), LAYER_SIZES):
            Ws.append(jax.random.normal(k, (prev * F, h), dtype=jnp.float32) * 0.01)
            prev = h
        return {'X0': X0, 'W0': Ws[0], 'W1': Ws[1], 'W2': Ws[2]}
    _L0_rec_all = _L0_rec_setup()
    _L0_rec_in = {k: v for k, v in _L0_rec_all.items() if k in ('W0', 'W1', 'W2')}
    del _L0_rec_all
    return {'dense_ctx': dense_ctx, 'ids': ids, 'tbl_0': tbl_0, 'tbl_1': tbl_1, 'tbl_2': tbl_2, 'tbl_3': tbl_3, 'tbl_4': tbl_4, 'tbl_5': tbl_5, 'tbl_6': tbl_6, 'tbl_7': tbl_7, 'tbl_8': tbl_8, 'tbl_9': tbl_9, 'tbl_10': tbl_10, 'tbl_11': tbl_11, 'tbl_12': tbl_12, 'tbl_13': tbl_13, 'tbl_14': tbl_14, 'tbl_15': tbl_15, 'tbl_16': tbl_16, 'tbl_17': tbl_17, 'tbl_18': tbl_18, 'tbl_19': tbl_19, 'tbl_20': tbl_20, 'tbl_21': tbl_21, 'tbl_22': tbl_22, 'tbl_23': tbl_23, 'W_top1': W_top1, 'b_top1': b_top1, 'W_top2': W_top2, 'b_top2': b_top2, 'W_top3': W_top3, 'L0_rec_W0': _L0_rec_in['W0'], 'L0_rec_W1': _L0_rec_in['W1'], 'L0_rec_W2': _L0_rec_in['W2']}

def reference(dense_ctx, ids, tbl_0, tbl_1, tbl_2, tbl_3, tbl_4, tbl_5, tbl_6, tbl_7, tbl_8, tbl_9, tbl_10, tbl_11, tbl_12, tbl_13, tbl_14, tbl_15, tbl_16, tbl_17, tbl_18, tbl_19, tbl_20, tbl_21, tbl_22, tbl_23, W_top1, b_top1, W_top2, b_top2, W_top3, L0_rec_W0, L0_rec_W1, L0_rec_W2):
    import jax
    import jax.numpy as jnp

    def _L0_rec_ref(X0, W0, W1, W2):
        import jax, jax.numpy as jnp
        import numpy as np
        B, F, D = (512, 24, 16)
        LAYER_SIZES = [64, 64, 64]

        def _cin_forward(X0, Ws):
            F_ = X0.shape[1]
            Xk = X0
            outs = []
            for W in Ws:
                H_prev = Xk.shape[1]
                Wr = W.reshape(F_, H_prev, W.shape[1])
                Xk = jnp.einsum('bfd,bhd,fho->bod', X0, Xk, Wr)
                outs.append(Xk.sum(axis=2))
            return jnp.concatenate(outs, axis=1)
        return _cin_forward(X0, (W0, W1, W2))
    e = jnp.stack([tbl_0[ids[:, 0]], tbl_1[ids[:, 1]], tbl_2[ids[:, 2]], tbl_3[ids[:, 3]], tbl_4[ids[:, 4]], tbl_5[ids[:, 5]], tbl_6[ids[:, 6]], tbl_7[ids[:, 7]], tbl_8[ids[:, 8]], tbl_9[ids[:, 9]], tbl_10[ids[:, 10]], tbl_11[ids[:, 11]], tbl_12[ids[:, 12]], tbl_13[ids[:, 13]], tbl_14[ids[:, 14]], tbl_15[ids[:, 15]], tbl_16[ids[:, 16]], tbl_17[ids[:, 17]], tbl_18[ids[:, 18]], tbl_19[ids[:, 19]], tbl_20[ids[:, 20]], tbl_21[ids[:, 21]], tbl_22[ids[:, 22]], tbl_23[ids[:, 23]]], axis=1)
    z = _L0_rec_ref(e, L0_rec_W0, L0_rec_W1, L0_rec_W2)
    z = z.reshape(z.shape[0], -1)
    h = jnp.concatenate([z, dense_ctx], axis=1)
    h = jnp.maximum(h @ W_top1 + b_top1, 0.0)
    h = jnp.maximum(h @ W_top2 + b_top2, 0.0)
    y = h @ W_top3
    return y

_drawn_inputs = setup_inputs


def setup_inputs(seed=0):
    import zlib

    import numpy as np

    out = dict(_drawn_inputs(seed))
    spreads = {'b_top1': (0.0, 0.1), 'b_top2': (0.0, 0.1)}
    factors = {'tbl_0': 8.0,
     'tbl_1': 8.0,
     'tbl_2': 8.0,
     'tbl_3': 8.0,
     'tbl_4': 8.0,
     'tbl_5': 8.0,
     'tbl_6': 8.0,
     'tbl_7': 8.0,
     'tbl_8': 8.0,
     'tbl_9': 8.0,
     'tbl_10': 8.0,
     'tbl_11': 8.0,
     'tbl_12': 8.0,
     'tbl_13': 8.0,
     'tbl_14': 8.0,
     'tbl_15': 8.0,
     'tbl_16': 8.0,
     'tbl_17': 8.0,
     'tbl_18': 8.0,
     'tbl_19': 8.0,
     'tbl_20': 8.0,
     'tbl_21': 8.0,
     'tbl_22': 8.0,
     'tbl_23': 8.0,
     'L0_rec_W0': 8.0,
     'L0_rec_W1': 8.0,
     'L0_rec_W2': 8.0}
    for name, (base, spread) in spreads.items():
        noise = np.random.default_rng([zlib.crc32(name.encode()), seed]).standard_normal(out[name].shape)
        drawn = base * np.exp(spread * noise) if base else spread * noise
        out[name] = jnp.asarray(drawn.astype(out[name].dtype))
    for name, factor in factors.items():
        out[name] = (out[name] * factor).astype(out[name].dtype)
    return out
```

```python
from contextlib import ExitStack

import numpy as np

import concourse.bass as bass
from concourse import mybir

B, F, D = 512, 24, 16
H = 64
PARTS = 3
XR = PARTS * F
TILES = B // 128
PAIRS = 2 * TILES
HB = 32
N = HB * D
LAST = TILES - 1
KD = F // 2 + 1
KC = 5
C1 = -(-KD // KC)
U2 = 4
V2 = 32
I2, J2 = F // U2, H // V2
K2 = I2 // 2
GB = 8
GP = HB // GB
GC = (F + 1) * GB
M1, M2 = 512, 256
Q1, Q2 = M1 // 128, M2 // 128


def dlrm_tower(nc, ids, tables, dense_t, w0a, w0b, w1, w2, wt1, bt1, wt2, bt2, wt3,
               sel_a1, sel_b1, sel_x0, sel_n, eye_f, eye_b, mask, out):
    f32, bf16, i32 = mybir.dt.float32, mybir.dt.bfloat16, mybir.dt.int32
    ALU, ACT, AX = mybir.AluOpType, mybir.ActivationFunctionType, mybir.AxisListType

    def seqno(p, pos):
        if isinstance(p, int) and p == -1:
            return pos - 1
        n = p * 5 + (pos + 2)
        return n - 2 if isinstance(p, int) and p == PAIRS - 1 and pos >= 3 else n

    def units(t):
        e, o = t * 2, t * 2 + 1
        if isinstance(t, int) and t == LAST:
            us = [(e, 1), (e, 2), (e, 3), (e, 4), (o, 0), (o, 3), (o, 4), None]
        else:
            n = t * 2 + 2
            us = [(e, 1), (e, 2), (e, 3), (e, 4)] + [(o, k) for k in range(5)] + [(n, 0), (n, 1), (n, 2)]
        names = ["e2", "e3", "e4"] + ["o%d" % u[1] for u in us[4:-1] if u[0] is o] + ["n0", "n1"]
        return [(names[i], us[i], us[i + 1], us[i + 2]) for i in range(len(us) - 2)]

    AUX6 = ["T0", "T1", "X0n_e", "X2T_e", "G1_e", "X0n_o", "X2T_o", "G1_o"]
    AUX7 = ["A1_e0", "A1_e1", "G0_e", "A1_o0", "A1_o1", "G0_o"]
    PRE6, PRE7 = 2, 4

    def aux6(t, name):
        last = isinstance(t, int) and t == LAST
        order = [x for x in AUX6 if not (last and x[0] == "T")]
        return t * len(AUX6) + (PRE6 + order.index(name) + 1)

    def aux7(t, name):
        last = isinstance(t, int) and t == LAST
        order = [x for x in AUX7 if not (last and x[0] == "A")]
        return t * len(AUX7) + (PRE7 + order.index(name) + 1)

    with ExitStack() as ctx:
        def sb(name, shape, dt=f32):
            return ctx.enter_context(nc.sbuf_tensor(name, shape, dt))

        def psum(name, shape):
            return ctx.enter_context(nc.psum_tensor(name, shape, f32))

        def sem(name):
            return ctx.enter_context(nc.semaphore(name))

        ids_sb = sb("ids_sb", [128, TILES, F], i32)
        w0a_sb = sb("w0a_sb", [128, C1, H])
        w0b_sb = sb("w0b_sb", [128, C1, H])
        w0_sb = sb("w0_sb", [128, C1, H])
        w1_sb = sb("w1_sb", [128, I2, J2, H])
        w2_sb = sb("w2_sb", [128, F, H])
        wt1a_sb = sb("wt1a_sb", [128, M1])
        wt1b_sb = sb("wt1b_sb", [H + D, M1])
        wt2_sb = sb("wt2_sb", [128, Q1, M2])
        wt3_sb = sb("wt3_sb", [128, Q2])
        bt1_sb = sb("bt1_sb", [128, Q1])
        bt2_sb = sb("bt2_sb", [128, Q2])
        sel_a1_sb = sb("sel_a1_sb", [XR, 128], bf16)
        sel_b1_sb = sb("sel_b1_sb", [XR, C1, 128], bf16)
        sel_x0_sb = sb("sel_x0_sb", [XR, I2, 128], bf16)
        sel_n_sb = sb("sel_n_sb", [XR, F], bf16)
        eye_f_sb = sb("eye_f_sb", [128, 128])
        eye_b_sb = sb("eye_b_sb", [128, 128], bf16)
        mask_sb = sb("mask_sb", [128, GB])
        emb = sb("emb", [128, TILES, F, D])
        rest = sb("rest", [128, D, F])
        parts = sb("parts", [128, D, PARTS, F], bf16)
        x0t = sb("x0t", [XR, PAIRS * 2 * N], bf16)
        a1 = sb("a1", [128, 2, 2, N])
        z1a = sb("z1a", [128, 2, 2, N])
        z1b = sb("z1b", [128, 2, N])
        bx = sb("bx", [128, 2, 2, J2, N])
        z2 = sb("z2", [128, K2, 2, J2, 2, N])
        x2_sb = sb("x2_sb", [128, N])
        x2t = sb("x2t", [128, GP, 128])
        bd = sb("bd", [128, 2 * GP, F + 1, GB])
        g_sb = sb("g_sb", [128, F + 1, PAIRS, HB])
        s1 = sb("s1", [128, PAIRS, HB])
        in_a = sb("in_a", [128, PAIRS, 2, HB])
        in_b = sb("in_b", [H + D, PAIRS, 2, HB])
        h1 = sb("h1", [128, Q1, B])
        h2 = sb("h2", [128, Q2, B])
        y_sb = sb("y_sb", [1, B])
        ring = psum("ring", [128, 2, 2, N])
        x1_ps = psum("x1_ps", [128, N])
        x2_ps = psum("x2_ps", [128, N])
        ps6 = psum("ps6", [128, N])
        ps7 = psum("ps7", [128, N])

        ids_in = sem("ids_in")
        consts_in = sem("consts_in")
        w0_in = sem("w0_in")
        w_in = sem("w_in")
        rows_landed = sem("rows_landed")
        split_step = sem("split_step")
        parts_ready = sem("parts_ready")
        w0_ready = sem("w0_ready")
        reps_ready = sem("reps_ready")
        z_ready = sem("z_ready")
        main_done = sem("main_done")
        s1_ready = sem("s1_ready")
        b_copied = sem("b_copied")
        b_ready = sem("b_ready")
        aux6_full, aux6_free = sem("aux6_full"), sem("aux6_free")
        aux7_full, aux7_free = sem("aux7_full"), sem("aux7_free")
        x0t_ready = sem("x0t_ready")
        a1_ready = sem("a1_ready")
        bd_ready = sem("bd_ready")
        sum_cols = sem("sum_cols")
        x2_copied = sem("x2_copied")
        x2t_ready = sem("x2t_ready")
        g_ready = sem("g_ready")
        z3_done = sem("z3_done")
        in_ready_v, in_ready_a = sem("in_ready_v"), sem("in_ready_a")
        h1_done = sem("h1_done")
        h1_ready_v, h1_ready_a = sem("h1_ready_v"), sem("h1_ready_a")
        h2_done = sem("h2_done")
        h2_ready_v, h2_ready_a = sem("h2_ready_v"), sem("h2_ready_a")
        y_done, y_ready, y_out = sem("y_done"), sem("y_ready"), sem("y_out")

        block = ctx.enter_context(nc.Block())

        @block.sync
        def _(sp):
            sp.dma_start(ids_sb[:], ids).then_inc(ids_in, 16)
            for dst, src in ((eye_b_sb, eye_b), (sel_a1_sb, sel_a1), (sel_b1_sb, sel_b1), (sel_x0_sb, sel_x0)):
                sp.dma_start(dst[:], src).then_inc(consts_in, 16)
            for dst, src in ((w0a_sb, w0a), (w0b_sb, w0b)):
                sp.dma_start(dst[:], src).then_inc(w0_in, 16)
            for dst, src in ((w1_sb[:], w1), (sel_n_sb[:], sel_n), (mask_sb[:], mask), (eye_f_sb[:], eye_f),
                             (w2_sb[0:H], w2), (w2_sb[H:2 * H], w2),
                             (wt1a_sb[:], wt1[0:128]), (wt1b_sb[:], wt1[128:2 * H + H + D]),
                             (wt2_sb[:], wt2), (wt3_sb[:], wt3), (bt1_sb[:], bt1), (bt2_sb[:], bt2),
                             (in_b[H:H + D].rearrange("p a s b -> p (a s b)"), dense_t)):
                sp.dma_start(dst, src).then_inc(w_in, 16)
            for p in range(PAIRS):
                if p:
                    sp.wait_ge(b_ready, 48 * p)
                sp.wait_ge(b_copied, p + 1)
                for u in range(1, U2):
                    sp.dma_start(bx[u * V2:(u + 1) * V2, p % 2], bx[0:V2, p % 2]).then_inc(b_ready, 16)
            sp.wait_ge(y_ready, 1)
            sp.dma_start(out, y_sb[:]).then_inc(y_out, 16)
            sp.wait_ge(y_out, 16)

        @block.gpsimd
        def _(pool):
            pool.wait_ge(ids_in, 16)
            for t in range(TILES):
                for f in range(F):
                    nc.gpsimd.indirect_dma_start(
                        out=emb[:, t, f, :], out_offset=None, in_=tables[f][:, :],
                        in_offset=bass.IndirectOffsetOnAxis(ap=ids_sb[:, t, f:f + 1], axis=0),
                    ).then_inc(rows_landed, 16)
                pool.wait_ge(rows_landed, 16 * F * (t + 1))

        @block.vector
        def _(dve):
            steps = [0]

            def chain(ins, base):
                steps[0] += 1
                ins.then_inc(split_step, 1)
                dve.wait_ge(split_step, base + steps[0])

            def split(t):
                steps[0] = 0
                base = t * 3
                dve.wait_ge(rows_landed, (t + 1) * (16 * F))
                if not (isinstance(t, int) and t == 0):
                    dve.wait_ge(x0t_ready, t * 2)
                e = emb[:, bass.ds(t, 1)].rearrange("p a f d -> p (a d) f") if not isinstance(t, int) else \
                    emb[:, t].rearrange("p f d -> p d f")
                chain(nc.vector.tensor_copy(parts[:, :, 0, :], e), base)
                chain(nc.vector.tensor_tensor(rest[:], e, parts[:, :, 0, :], ALU.subtract), base)
                chain(nc.vector.tensor_copy(parts[:, :, 1, :], rest[:]), base)
                nc.vector.tensor_tensor(parts[:, :, 2, :], rest[:], parts[:, :, 1, :],
                                        ALU.subtract).then_inc(parts_ready, 1)

            def products(p, pos, s, parity, wait_free):
                n = seqno(p, pos)
                if s == 0:
                    if wait_free:
                        dve.wait_ge(main_done, seqno(p - 1, 4 if pos == 2 else pos) + 1)
                    if pos == 0:
                        dve.wait_ge(b_copied, p + 1)
                        dve.wait_ge(b_ready, p * 48 + 48)
                    if pos == 1:
                        dve.wait_ge(a1_ready, p * 2 + 4)
                dve.wait_ge(reps_ready, n * 2 + (s + 1))
                shape = [128, J2, 2, N]
                if pos == 1:
                    q = 1 - parity
                    left = a1[:, q, s, :].rearrange("p (a n) -> p a n", a=1).to_broadcast([128, 2, N])
                    nc.vector.tensor_tensor(z1a[:, s], ring[:, s], left, ALU.mult).then_inc(z_ready, 1)
                elif pos == 2:
                    nc.vector.tensor_tensor(z1b[:, s], ring[:, s, 0], a1[:, 1 - parity, s], ALU.mult)\
                        .then_inc(z_ready, 1)
                else:
                    k = 0 if pos == 0 else pos - 2
                    x0 = ring[:, s].rearrange("p (a i) n -> p a i n", a=1).to_broadcast(shape)
                    x1 = bx[:, parity, s].rearrange("p j (a n) -> p j a n", a=1).to_broadcast(shape)
                    nc.vector.tensor_tensor(z2[:, k, s], x0, x1, ALU.mult).then_inc(z_ready, 1)

            def sum_x1(p, at):
                dve.wait_ge(b_copied, p + 1)
                nc.vector.reduce_sum(at, x1_ps[:].rearrange("p (d b) -> p b d", b=HB), AX.X).then_inc(s1_ready, 1)

            def s1_at(p):
                return s1[:, p] if isinstance(p, int) else s1[:, bass.ds(p, 1)].rearrange("p a b -> p (a b)")

            def tile(t, last):
                for name, prev, (p, pos), nxt in units(t):
                    parity = 1 if name[0] == "o" else 0
                    for s in range(2):
                        products(p, pos, s, parity, True)
                        if s == 0 and name == "e4":
                            sum_x1(t * 2 + 1, s1_at(t * 2 + 1))
                        if s == 0 and name == "o4" and not last:
                            sum_x1(t * 2 + 2, s1_at(t * 2 + 2))
                    if name == "e3" and not last:
                        split(t + 1)

            dve.wait_ge(w_in, 16 * 13)
            for q in range(2 * GP):
                last_col = nc.vector.tensor_copy(bd[:, q, F, :], mask_sb[:])
            last_col.then_inc(sum_cols, 1)
            dve.wait_ge(w0_in, 32)
            nc.vector.tensor_tensor(w0_sb[:], w0a_sb[:], w0b_sb[:], ALU.add).then_inc(w0_ready, 1)
            split(0)
            for pos in (1, 2):
                for s in range(2):
                    products(-1, pos, s, 1, False)
            sum_x1(0, s1_at(0))
            for pos in (0, 1):
                for s in range(2):
                    products(0, pos, s, 0, pos == 1)
            with dve.Fori(0, LAST) as t:
                tile(t, False)
            tile(LAST, True)

            for s in range(2):
                nc.vector.tensor_copy(in_a[0:H, :, s, :], s1[s * H:(s + 1) * H])
            dve.wait_ge(g_ready, 2 * PAIRS)
            for s in range(2):
                cp = nc.vector.tensor_copy(in_a[H:2 * H, :, s, :], g_sb[s * H:(s + 1) * H, F])
            cp.then_inc(in_ready_v, 1)
            for q in range(1, Q1, 2):
                dve.wait_ge(h1_done, q + 1)
                nc.vector.tensor_scalar(h1[:, q], ring[:, q // 2, q % 2], bt1_sb[:, q:q + 1], 0.0,
                                        ALU.add, ALU.max).then_inc(h1_ready_v, 1)
            dve.wait_ge(h2_done, 2)
            nc.vector.tensor_scalar(h2[:, 1], x2_ps[:], bt2_sb[:, 1:2], 0.0, ALU.add, ALU.max)\
                .then_inc(h2_ready_v, 1)
            dve.wait_ge(y_done, 1)
            nc.vector.tensor_copy(y_sb[:], ps6[0:1, :]).then_inc(y_ready, 1)

        @block.tensor
        def _(pe):
            def cols(p, s):
                return x0t[:, p * (2 * N) + s * N:p * (2 * N) + (s + 1) * N] if isinstance(p, int) else \
                    x0t[:, bass.ds(p * (2 * N) + s * N, N)]

            def select(dst, sel, p, s):
                return nc.tensor.matmul(dst, sel, cols(p, s), start=True, stop=True)

            def reps(p, pos, s):
                n = seqno(p, pos)
                if not (isinstance(p, int) and p == -1 and pos == 1):
                    pe.wait_ge(z_ready, n * 2 + (s - 1))
                if pos == 1:
                    for c in range(2):
                        mm = select(ring[:, s, c], sel_b1_sb[:, c], p + 1, s)
                elif pos == 2:
                    mm = select(ring[:, s, 0], sel_b1_sb[:, 2], p + 1, s)
                else:
                    k = 0 if pos == 0 else pos - 2
                    for i in range(2):
                        mm = select(ring[:, s, i], sel_x0_sb[:, 2 * k + i], p, s)
                mm.then_inc(reps_ready, 1)

            def main(p, pos, half):
                n = seqno(p, pos)
                if half == 0:
                    pe.wait_ge(z_ready, n * 2 + 2)
                    if pos == 0 and not (isinstance(p, int) and p == 0):
                        pe.wait_ge(x2_copied, p * 1)
                    if pos == 1 and not (isinstance(p, int) and p == -1):
                        pe.wait_ge(b_copied, p + 1)
                        pe.wait_ge(s1_ready, p + 1)
                if pos == 1:
                    todo = [(w0_sb[:, half], lambda s: z1a[:, s, half], half == 0, False)]
                elif pos == 2:
                    todo = [(w0_sb[:, 2], lambda s: z1b[:, s], False, True)] if half == 0 else []
                else:
                    k = 0 if pos == 0 else pos - 2
                    todo = [(w1_sb[:, 2 * k + i, half], lambda s, i=i: z2[:, k, s, half, i],
                             (k, half, i) == (0, 0, 0), (k, half, i) == (K2 - 1, 1, 1)) for i in range(2)]
                acc = x1_ps if pos in (1, 2) else x2_ps
                for w, z, first, final in todo:
                    for s in range(2):
                        mm = nc.tensor.matmul(acc[s * H:(s + 1) * H, :], w, z(s), start=first, stop=final)
                if half == (0 if pos == 2 else 1):
                    mm.then_inc(main_done, 1)

            def transposes(t_parts, part, count):
                if part == 0:
                    pe.wait_ge(parts_ready, t_parts)
                if not (isinstance(count, int) and count == 1):
                    pe.wait_ge(aux6_free, count - 1)
                for d in range(8):
                    tp = nc.tensor.transpose(ps6[:].bitcast(bf16)[0:XR, d * 128:(d + 1) * 128],
                                             parts[:, 8 * part + d].rearrange("p a f -> p (a f)"), eye_b_sb[:])
                tp.then_inc(aux6_full, 1)

            def left_factor(p, s, count, tiles_in):
                pe.wait_ge(x0t_ready, tiles_in)
                if not (isinstance(count, int) and count == 1):
                    pe.wait_ge(aux7_free, count - 1)
                select(ps7[:], sel_a1_sb[:], p, s).then_inc(aux7_full, 1)

            def x0_by_column(p, count):
                pe.wait_ge(aux6_free, count - 1)
                for s in range(2):
                    for g in range(GP):
                        by_group = x0t[:].rearrange("r (m g) -> r g m", g=GP)[:, g]
                        at = p * (2 * 128) + s * 128
                        c = by_group[:, at:at + 128] if isinstance(p, int) else by_group[:, bass.ds(at, 128)]
                        q = s * GP + g
                        mm = nc.tensor.matmul(ps6[:, q * F:(q + 1) * F], c, sel_n_sb[:], start=True, stop=True)
                mm.then_inc(aux6_full, 1)

            def x2_by_column(p, count):
                pe.wait_ge(x2_copied, p + 1)
                pe.wait_ge(aux6_free, count - 1)
                for g in range(GP):
                    c = x2_sb[:].rearrange("r (m g) -> r g m", g=GP)[:, g]
                    tp = nc.tensor.transpose(ps6[:, g * 128:(g + 1) * 128], c, eye_f_sb[:])
                tp.then_inc(aux6_full, 1)

            def outer_sums(p, count6, count7):
                pe.wait_ge(x2t_ready, p + 1)
                pe.wait_ge(bd_ready, p + 1)
                for g in range(GP):
                    if g == 0:
                        pe.wait_ge(aux7_free, count7 - 1)
                    if g == 2:
                        pe.wait_ge(aux6_free, count6 - 1)
                    bank = (ps7, ps6)[g // 2]
                    at = (g % 2) * GC
                    for s in range(2):
                        mm = nc.tensor.matmul(bank[s * H:(s + 1) * H, at:at + GC], x2t[:, g, s * H:(s + 1) * H],
                                              bd[:, s * GP + g].rearrange("p f b -> p (f b)"),
                                              start=True, stop=True)
                    if g == 1:
                        mm.then_inc(aux7_full, 1)
                    if g == 3:
                        mm.then_inc(aux6_full, 1)

            def tile(t, last):
                e, o = t * 2, t * 2 + 1
                for name, prev, u, nxt in units(t):
                    reps(*u, 1)
                    if not last:
                        if name == "e4":
                            transposes(t + 2, 0, aux6(t, "T0"))
                        if name == "o0":
                            left_factor(t * 2 + 2, 0, aux7(t, "A1_e0"), t * 2 + 4)
                    if name == "o0":
                        x0_by_column(e, aux6(t, "X0n_e"))
                    if name == "n0" :
                        x0_by_column(o, aux6(t, "X0n_o"))
                    main(*prev, 0)
                    if not last:
                        if name == "e4":
                            transposes(t + 2, 1, aux6(t, "T1"))
                        if name == "o0":
                            left_factor(t * 2 + 2, 1, aux7(t, "A1_e1"), t * 2 + 4)
                        if name == "o3":
                            left_factor(t * 2 + 3, 0, aux7(t, "A1_o0"), t * 2 + 4)
                        if name == "o4":
                            left_factor(t * 2 + 3, 1, aux7(t, "A1_o1"), t * 2 + 4)
                    if name == ("o3" if last else "o1"):
                        x2_by_column(e, aux6(t, "X2T_e"))
                    if name == "n1":
                        x2_by_column(o, aux6(t, "X2T_o"))
                    if nxt:
                        reps(*nxt, 0)
                    main(*prev, 1)
                    if name == ("o3" if last else "o1"):
                        outer_sums(e, aux6(t, "G1_e"), aux7(t, "G0_e"))
                    if name == "n1":
                        outer_sums(o, aux6(t, "G1_o"), aux7(t, "G0_o"))

            pe.wait_ge(consts_in, 16 * 4)
            transposes(1, 0, 1)
            transposes(1, 1, 2)
            left_factor(0, 0, 1, 2)
            left_factor(0, 1, 2, 2)
            for s in range(2):
                reps(-1, 1, s)
            reps(-1, 2, 0)
            reps(-1, 2, 1)
            pe.wait_ge(w0_ready, 1)
            for pos in (1, 2):
                main(-1, pos, 0)
                main(-1, pos, 1)
            left_factor(1, 0, 3, 2)
            left_factor(1, 1, 4, 2)
            reps(0, 0, 0)
            reps(0, 0, 1)
            reps(0, 1, 0)
            reps(0, 1, 1)
            pe.wait_ge(w_in, 16 * 13)
            main(0, 0, 0)
            reps(0, 2, 0)
            main(0, 0, 1)
            with pe.Fori(0, LAST) as t:
                tile(t, False)
            tile(LAST, True)
            p = PAIRS - 1
            x0_by_column(p, aux6(LAST, "X0n_o"))
            main(p, 4, 0)
            main(p, 4, 1)
            x2_by_column(p, aux6(LAST, "X2T_o"))
            outer_sums(p, aux6(LAST, "G1_o"), aux7(LAST, "G0_o"))

            pe.wait_ge(g_ready, 2 * PAIRS)
            for f in range(F):
                for s, bank in enumerate((x1_ps, x2_ps)):
                    mm = nc.tensor.matmul(bank[s * H:(s + 1) * H, 0:PAIRS * HB], w2_sb[s * H:(s + 1) * H, f],
                                          g_sb[s * H:(s + 1) * H, f].rearrange("p a b -> p (a b)"),
                                          start=(f == 0), stop=(f == F - 1))
            mm.then_inc(z3_done, 1)

            pe.wait_ge(in_ready_v, 1)
            for q in range(Q1):
                nc.tensor.matmul(ring[:, q // 2, q % 2], wt1a_sb[:, q * 128:(q + 1) * 128],
                                 in_a[:].rearrange("p a s b -> p (a s b)"), start=True, stop=False)
            pe.wait_ge(in_ready_a, 2)
            for q in range(Q1):
                nc.tensor.matmul(ring[:, q // 2, q % 2], wt1b_sb[:, q * 128:(q + 1) * 128],
                                 in_b[:].rearrange("p a s b -> p (a s b)"), start=False, stop=True)\
                    .then_inc(h1_done, 1)
            for m, bank in enumerate((x1_ps, x2_ps)):
                for q in range(Q1):
                    if m == 0:
                        pe.wait_ge((h1_ready_a, h1_ready_v)[q % 2], q // 2 + 1)
                    mm = nc.tensor.matmul(bank[:], wt2_sb[:, q, m * 128:(m + 1) * 128], h1[:, q],
                                          start=(q == 0), stop=(q == Q1 - 1))
                mm.then_inc(h2_done, 1)
            for m in range(Q2):
                pe.wait_ge((h2_ready_a, h2_ready_v)[m], 1)
                mm = nc.tensor.matmul(ps6[0:1, :], wt3_sb[:, m:m + 1], h2[:, m], start=(m == 0), stop=(m == Q2 - 1))
            mm.then_inc(y_done, 1)

        @block.scalar
        def _(act):
            def copy(dst, src):
                return nc.scalar.activation(dst, src, ACT.Copy)

            def x0t_copy(t, part, count):
                act.wait_ge(aux6_full, count)
                if isinstance(t, int):
                    dst = x0t[:, t * 4 * N:(t + 1) * 4 * N]
                else:
                    dst = x0t[:, bass.ds(t * (4 * N), 4 * N)]
                dst = dst.rearrange("r (q d b) -> r q d b", q=4, b=HB)[:, :, 8 * part:8 * part + 8]
                src = ps6[:].bitcast(bf16)[0:XR, :].rearrange("r (d q b) -> r q d b", q=4, b=HB)
                for q in range(4):
                    cp = copy(dst[:, q], src[:, q])
                cp.then_inc(aux6_free, 1)
                act.wait_ge(aux6_free, count)
                act.sem_inc(x0t_ready, 1)

            def a1_copy(parity, s, count, free):
                act.wait_ge(aux7_full, count)
                if free is not None:
                    act.wait_ge(z_ready, free)
                copy(a1[:, parity, s], ps7[:]).then_inc(aux7_free, 1)
                act.wait_ge(aux7_free, count)
                act.sem_inc(a1_ready, 1)

            def b_copy(p, parity, free):
                act.wait_ge(main_done, seqno(p - 1, 2) + 1)
                if free is not None:
                    act.wait_ge(z_ready, free)
                for s in range(2):
                    for j in range(J2):
                        at = s * H + j * V2
                        cp = copy(bx[0:V2, parity, s, j], x1_ps[at:at + V2, :])
                cp.then_inc(b_copied, 1)

            def bd_build(t, p, name):
                act.wait_ge(aux6_full, aux6(t, name))
                for b in range(GB):
                    cp = nc.scalar.activation(bd[:, :, 0:F, b], ps6[:, 0:2 * GP * F].rearrange("p (q f) -> p q f", f=F),
                                              ACT.Copy, scale=mask_sb[:, b:b + 1])
                cp.then_inc(aux6_free, 1)
                act.wait_ge(aux6_free, aux6(t, name))
                act.sem_inc(bd_ready, 1)

            def x2_copy(p, pos_done):
                act.wait_ge(main_done, pos_done)
                copy(x2_sb[:], x2_ps[:]).then_inc(x2_copied, 1)

            def x2t_copy(t, name):
                act.wait_ge(aux6_full, aux6(t, name))
                copy(x2t[:].rearrange("p g c -> p (g c)"), ps6[:]).then_inc(aux6_free, 1)
                act.wait_ge(aux6_free, aux6(t, name))
                act.sem_inc(x2t_ready, 1)

            def g_copy(t, p, odd):
                x = "eo"[odd]
                for part, (bank, full, free, count) in enumerate((
                        (ps7, aux7_full, aux7_free, aux7(t, "G0_" + x)), (ps6, aux6_full, aux6_free, aux6(t, "G1_" + x)))):
                    act.wait_ge(full, count)
                    src = bank[:, 0:2 * GC].rearrange("p (g f b) -> p f b g", g=2, b=GB)
                    dst = g_sb[:].rearrange("p f a (b g) -> p f (a b) g", g=GP)
                    dst = dst[:, :, p * GB:(p + 1) * GB] if isinstance(p, int) else dst[:, :, bass.ds(p * GB, GB)]
                    dst = dst[:, :, :, 2 * part:2 * part + 2]
                    copy(dst, src).then_inc(free, 1)
                    act.wait_ge(free, count)
                    act.sem_inc(g_ready, 1)

            def tile(t, last):
                e, o = t * 2, t * 2 + 1
                b_copy(o, 1, (seqno(o - 2, 4) + 1) * 2)
                if not last:
                    x0t_copy(t + 1, 0, aux6(t, "T0"))
                    x0t_copy(t + 1, 1, aux6(t, "T1"))
                    a1_copy(0, 0, aux7(t, "A1_e0"), None)
                bd_build(t, e, "X0n_e")
                if not last:
                    a1_copy(0, 1, aux7(t, "A1_e1"), None)
                x2_copy(e, seqno(e, 4) + 1)
                x2t_copy(t, "X2T_e")
                g_copy(t, e, 0)
                if not last:
                    a1_copy(1, 0, aux7(t, "A1_o0"), None)
                    b_copy(t * 2 + 2, 0, (seqno(e, 4) + 1) * 2)
                    a1_copy(1, 1, aux7(t, "A1_o1"), None)
                bd_build(t, o, "X0n_o")
                x2_copy(o, seqno(o, 4) + 1)
                x2t_copy(t, "X2T_o")
                g_copy(t, o, 1)

            x0t_copy(0, 0, 1)
            x0t_copy(0, 1, 2)
            for s in range(2):
                a1_copy(0, s, 1 + s, None)
            b_copy(0, 0, None)
            for s in range(2):
                a1_copy(1, s, 3 + s, None)
            act.wait_ge(w_in, 16 * 13)
            act.wait_ge(sum_cols, 1)
            with act.Fori(0, LAST) as t:
                tile(t, False)
            tile(LAST, True)

            act.wait_ge(z3_done, 1)
            for s, bank in enumerate((x1_ps, x2_ps)):
                copy(in_b[0:H, :, s, :], bank[s * H:(s + 1) * H, 0:PAIRS * HB].rearrange("p (a b) -> p a b", b=HB))\
                    .then_inc(in_ready_a, 1)
            for q in range(0, Q1, 2):
                act.wait_ge(h1_done, q + 1)
                nc.scalar.activation(h1[:, q], ring[:, q // 2, q % 2], ACT.Relu, bias=bt1_sb[:, q:q + 1])\
                    .then_inc(h1_ready_a, 1)
            act.wait_ge(h2_done, 1)
            nc.scalar.activation(h2[:, 0], x1_ps[:], ACT.Relu, bias=bt2_sb[:, 0:1]).then_inc(h2_ready_a, 1)


def _field_pairs():
    rows = []
    for c in range(C1):
        for p in range(128):
            k, f = c * KC + p // F, p % F
            ok = p < KC * F and (k < KD - 1 or (k == KD - 1 and f < F // 2))
            rows.append((f, (f + k) % F) if ok else None)
    return rows


def kernel(**inputs):
    import ml_dtypes
    import concourse.bacc as _bacc
    from concourse.bass_utils import run_bass_kernel_spmd as _run

    x = {k: np.asarray(v) for k, v in inputs.items()}
    bf = ml_dtypes.bfloat16
    w0 = x["L0_rec_W0"]
    w0a = np.zeros((C1 * 128, H), w0.dtype)
    w0b = np.zeros((C1 * 128, H), w0.dtype)
    sel_b1 = np.zeros((F, C1, 128), bf)
    for r, fh in enumerate(_field_pairs()):
        if fh is None:
            continue
        f, h = fh
        w0a[r] = w0[f * F + h]
        if f != h:
            w0b[r] = w0[h * F + f]
        sel_b1[h, r // 128, r % 128] = 1
    by_block = lambda w: np.ascontiguousarray(w.reshape(C1, 128, H).transpose(1, 0, 2))
    w1 = x["L0_rec_W1"].reshape(I2, U2, J2, V2, H).transpose(1, 3, 0, 2, 4).reshape(128, I2, J2, H)
    w2 = x["L0_rec_W2"].reshape(F, H, H).transpose(1, 0, 2)
    sel_a1 = np.zeros((F, 128), bf)
    sel_x0 = np.zeros((F, I2, 128), bf)
    for p in range(KC * F):
        sel_a1[p % F, p] = 1
    for i in range(I2):
        for p in range(128):
            sel_x0[U2 * i + p // V2, i, p] = 1
    three = lambda a: np.concatenate([a] * PARTS, axis=0)
    mask = np.zeros((128, GB), np.float32)
    for p in range(128):
        mask[p, p % GB] = 1
    arrays = {
        "ids": x["ids"].reshape(TILES, 128, F).transpose(1, 0, 2),
        "dense_t": x["dense_ctx"].T,
        "w0a": by_block(w0a), "w0b": by_block(w0b), "w1": w1, "w2": w2,
        "wt1": x["W_top1"], "bt1": x["b_top1"].reshape(Q1, 128).T,
        "wt2": x["W_top2"].reshape(Q1, 128, M2).transpose(1, 0, 2), "bt2": x["b_top2"].reshape(Q2, 128).T,
        "wt3": x["W_top3"].reshape(Q2, 128).T,
        "sel_a1": three(sel_a1), "sel_b1": three(sel_b1), "sel_x0": three(sel_x0),
        "sel_n": three(np.eye(F, dtype=bf)), "eye_f": np.eye(128, dtype=np.float32),
        "eye_b": np.eye(128, dtype=bf), "mask": mask,
    }
    for f in range(F):
        arrays[f"tbl_{f}"] = x[f"tbl_{f}"]
    arrays = {k: np.ascontiguousarray(v) for k, v in arrays.items()}

    nc = _bacc.Bacc("TRN2", target_bir_lowering=False, num_devices=1)
    aps = {k: nc.dram_tensor(k, v.shape, mybir.dt.from_np(v.dtype), kind="ExternalInput").ap()
           for k, v in arrays.items()}
    out = nc.dram_tensor("y", (B, 1), mybir.dt.float32, kind="ExternalOutput").ap()
    tables = [aps.pop(f"tbl_{f}") for f in range(F)]
    dlrm_tower(nc, tables=tables, out=out.rearrange("b o -> o b"), **aps)
    r = _run(nc, [arrays], core_ids=[0])
    return r.results[0]["y"]
```

```python
from contextlib import ExitStack

import numpy as np

import concourse.bass as bass
from concourse import mybir

B, F, D = 512, 24, 16
H = 64
PARTS = 3
XR = PARTS * F
TILES = B // 128
PAIRS = 2 * TILES
HB = 32
N = HB * D
LAST = TILES - 1
KD = F // 2 + 1
KC = 5
C1 = -(-KD // KC)
U2 = 8
V2 = 16
I2, J2 = F // U2, H // V2
QH = H // 32
GB = 8
GP = HB // GB
GC = (F + 1) * GB
M1, M2 = 512, 256
Q1, Q2 = M1 // 128, M2 // 128
WARM = 40


def dlrm_tower(nc, ids, tables, dense_t, w0a, w0b, w1, w2, wt1, bt1, wt2, bt2, wt3,
               sel_a1, sel_b1, sel_x0, sel_n, eye_f, eye_b, mask, out):
    f32, bf16, i32 = mybir.dt.float32, mybir.dt.bfloat16, mybir.dt.int32
    ALU, ACT, AX = mybir.AluOpType, mybir.ActivationFunctionType, mybir.AxisListType

    L1_OPS, OPS = 3, 3 + 2 * I2
    SLOTS = [(0, 1), (2, 3), (0, 1), (2,), (3,), (0,), (1,), (2,), (3,)]

    def ops(p, idx):
        if isinstance(p, int) and p == -1:
            return idx + 1
        n = p * OPS + (idx + L1_OPS + 1)
        return n - L1_OPS if isinstance(p, int) and p == PAIRS - 1 else n

    def slot_free(p, idx):
        first, last = isinstance(p, int) and p <= 0, isinstance(p, int) and p == PAIRS - 1
        if idx in (0, 1):
            if first:
                return None if p == -1 else ops(-1, 2)
            return ops(p - 1, (6, 8)[idx])
        if idx == 2:
            return ops(p, 0)
        if idx in (3, 4):
            return ops(p - 1, 8) if last else ops(p, 1)
        if idx in (5, 6):
            return ops(p - 1, 6) if last else ops(p, 2)
        return ops(p, idx - 4)

    AUX6 = ["T1", "X0n_e", "X2T_e", "G1_e", "X0n_o", "X2T_o", "G1_o"]
    AUX7 = ["T0", "A1_e0", "A1_e1", "G0_e", "A1_o0", "A1_o1", "G0_o"]
    PRE6, PRE7 = 3, 3
    B_COPIES = 16 * 3

    def aux6(t, name):
        order = [x for x in AUX6 if x[0] != "T"] if isinstance(t, int) else AUX6
        return t * len(AUX6) + (PRE6 + order.index(name) + 1)

    def aux7(t, name):
        order = [x for x in AUX7 if x[0] == "G"] if isinstance(t, int) else AUX7
        return t * len(AUX7) + (PRE7 + order.index(name) + 1)

    with ExitStack() as ctx:
        def sb(name, shape, dt=f32):
            return ctx.enter_context(nc.sbuf_tensor(name, shape, dt))

        def psum(name, shape):
            return ctx.enter_context(nc.psum_tensor(name, shape, f32))

        def sem(name):
            return ctx.enter_context(nc.semaphore(name))

        ids_sb = sb("ids_sb", [128, TILES, F], i32)
        w0a_sb = sb("w0a_sb", [128, C1, H])
        w0b_sb = sb("w0b_sb", [128, C1, H])
        w0_sb = sb("w0_sb", [128, C1, H])
        w1_sb = sb("w1_sb", [128, I2, J2, H])
        w2_sb = sb("w2_sb", [128, F, H])
        wt1a_sb = sb("wt1a_sb", [128, M1])
        wt1b_sb = sb("wt1b_sb", [H + D, M1])
        wt2_sb = sb("wt2_sb", [128, Q1, M2])
        wt3_sb = sb("wt3_sb", [128, Q2])
        bt1_sb = sb("bt1_sb", [128, Q1])
        bt2_sb = sb("bt2_sb", [128, Q2])
        sel_a1_sb = sb("sel_a1_sb", [XR, 128], bf16)
        sel_b1_sb = sb("sel_b1_sb", [XR, C1, 128], bf16)
        sel_x0_sb = sb("sel_x0_sb", [XR, I2, 128], bf16)
        sel_n_sb = sb("sel_n_sb", [XR, F], bf16)
        eye_f_sb = sb("eye_f_sb", [128, 128])
        eye_b_sb = sb("eye_b_sb", [128, 128], bf16)
        mask_sb = sb("mask_sb", [128, GB])
        emb = sb("emb", [128, TILES, F, D])
        rest = sb("rest", [128, D, F])
        parts = sb("parts", [128, D, PARTS, F], bf16)
        x0t = sb("x0t", [XR, PAIRS * 2 * N], bf16)
        a1 = sb("a1", [128, 2, 2, N])
        z1a = sb("z1a", [128, 2, 2, N])
        z1b = sb("z1b", [128, 2, N])
        x1q = sb("x1q", [32, 2, QH, N])
        bx = sb("bx", [128, 2, 2, J2, N])
        z2 = sb("z2", [128, I2, 2, J2, N])
        x2_sb = sb("x2_sb", [128, N])
        x2t = sb("x2t", [128, GP, 128])
        bd = sb("bd", [128, 2 * GP, F + 1, GB])
        g_sb = sb("g_sb", [128, F + 1, PAIRS, HB])
        s1 = sb("s1", [128, PAIRS, HB])
        in_a = sb("in_a", [128, PAIRS, 2, HB])
        in_b = sb("in_b", [H + D, PAIRS, 2, HB])
        h1 = z2[:, 0, 0]
        h2 = z2[:, 0, 1, 0:Q2]
        y_sb = sb("y_sb", [1, B])
        ring = psum("ring", [128, 4, N])
        x1_ps = psum("x1_ps", [128, N])
        x2_ps = psum("x2_ps", [128, N])
        ps6 = psum("ps6", [128, N])
        ps7 = psum("ps7", [128, N])

        ids_in = sem("ids_in")
        consts_in = sem("consts_in")
        w0_in = sem("w0_in")
        w_in = sem("w_in")
        gathers_issued = sem("gathers_issued")
        rows_landed = sem("rows_landed")
        split_step = sem("split_step")
        parts_ready = sem("parts_ready")
        w0_ready = sem("w0_ready")
        reps_ready = sem("reps_ready")
        z_ready = sem("z_ready")
        x1_done = sem("x1_done")
        l2_done = sem("l2_done")
        s1_ready = sem("s1_ready")
        b_copied = sem("b_copied")
        b_quadrant = sem("b_quadrant")
        b_ready = sem("b_ready")
        aux6_full, aux6_free = sem("aux6_full"), sem("aux6_free")
        aux7_full, aux7_free = sem("aux7_full"), sem("aux7_free")
        x0t_ready = sem("x0t_ready")
        x0t_half = sem("x0t_half")
        a1_ready = sem("a1_ready")
        bd_ready = sem("bd_ready")
        sum_cols = sem("sum_cols")
        x2_copied = sem("x2_copied")
        x2t_ready = sem("x2t_ready")
        g_ready = sem("g_ready")
        z3_done = sem("z3_done")
        in_ready_v, in_ready_a = sem("in_ready_v"), sem("in_ready_a")
        z3_ready = sem("z3_ready")
        h1_done = sem("h1_done")
        h1_ready_v, h1_ready_a = sem("h1_ready_v"), sem("h1_ready_a")
        h2_done = sem("h2_done")
        h2_ready_v, h2_ready_a = sem("h2_ready_v"), sem("h2_ready_a")
        y_done, y_ready, y_out = sem("y_done"), sem("y_ready"), sem("y_out")

        block = ctx.enter_context(nc.Block())

        def split(builder, engine, e, t):
            hi, mid, lo = (parts[:, :, k, :] for k in range(PARTS))
            builder.tensor_copy(hi, e).then_inc(split_step, 1)
            engine.wait_ge(split_step, 3 * t + 1)
            builder.tensor_tensor(rest[:], e, hi, ALU.subtract).then_inc(split_step, 1)
            engine.wait_ge(split_step, 3 * t + 2)
            builder.tensor_copy(mid, rest[:]).then_inc(split_step, 1)
            engine.wait_ge(split_step, 3 * t + 3)
            builder.tensor_tensor(lo, rest[:], mid, ALU.subtract).then_inc(parts_ready, 1)

        def x0t_pieces(t, part, bank):
            at = x0t[:, t * 4 * N:(t + 1) * 4 * N] if isinstance(t, int) else x0t[:, bass.ds(t * (4 * N), 4 * N)]
            dst = at.rearrange("r (q d b) -> r q d b", q=4, b=HB)[:, :, 8 * part:8 * part + 8]
            src = bank[:].bitcast(bf16)[0:XR, :].rearrange("r (d q b) -> r q d b", q=4, b=HB)
            return [(dst[:, q], src[:, q]) for q in range(4)]

        @block.sync
        def _(sp):
            sp.dma_start(ids_sb[:], ids).then_inc(ids_in, 16)
            for dst, src in ((eye_b_sb, eye_b), (sel_a1_sb, sel_a1), (sel_b1_sb, sel_b1), (sel_x0_sb, sel_x0)):
                sp.dma_start(dst[:], src).then_inc(consts_in, 16)
            for dst, src in ((w0a_sb, w0a), (w0b_sb, w0b)):
                sp.dma_start(dst[:], src).then_inc(w0_in, 16)
            for dst, src in ((w1_sb[:], w1), (sel_n_sb[:], sel_n), (mask_sb[:], mask), (eye_f_sb[:], eye_f),
                             (w2_sb[0:H], w2), (w2_sb[H:2 * H], w2),
                             (wt1a_sb[:], wt1[0:128]), (wt1b_sb[:], wt1[128:2 * H + H + D]),
                             (wt2_sb[:], wt2), (wt3_sb[:], wt3), (bt1_sb[:], bt1), (bt2_sb[:], bt2),
                             (in_b[H:H + D].rearrange("p a s b -> p (a s b)"), dense_t)):
                sp.dma_start(dst, src).then_inc(w_in, 16)
            for p in range(PAIRS):
                if p:
                    sp.wait_ge(b_ready, B_COPIES * p)
                if p >= 2:
                    sp.wait_ge(z_ready, ops(p - 2, OPS - 1))
                sp.wait_ge(b_copied, p + 1)
                for half in range(2):
                    for u in range(2):
                        sp.dma_start(bx[u * V2:(u + 1) * V2, p % 2, :, half::2], x1q[half * V2:(half + 1) * V2])\
                            .then_inc(b_quadrant, 16)
                sp.wait_ge(b_quadrant, 64 * (p + 1))
                for q in range(1, 4):
                    sp.dma_start(bx[32 * q:32 * (q + 1), p % 2], bx[0:32, p % 2]).then_inc(b_ready, 16)
            sp.wait_ge(y_ready, 1)
            sp.dma_start(out, y_sb[:]).then_inc(y_out, 16)
            sp.wait_ge(y_out, 16)

        @block.gpsimd
        def _(pool):
            pool.wait_ge(ids_in, 16)
            for t in range(TILES):
                for f in range(F):
                    nc.gpsimd.indirect_dma_start(
                        out=emb[:, t, f, :], out_offset=None, in_=tables[f][:, :],
                        in_offset=bass.IndirectOffsetOnAxis(ap=ids_sb[:, t, f:f + 1], axis=0),
                    ).then_inc(rows_landed, 16)
                    if (t, f) == (0, F - 4):
                        pool.sem_inc(gathers_issued, 1)
                pool.wait_ge(rows_landed, 16 * F * (t + 1))
                if t:
                    pool.wait_ge(x0t_ready, 2 * t)
                    split(nc.gpsimd, pool, emb[:, t].rearrange("p f d -> p d f"), t)

        @block.vector
        def _(dve):
            def layer1(p, idx, q):
                if idx == 0:
                    if not (isinstance(p, int) and p == -1):
                        dve.wait_ge(x1_done, p + 1)
                    dve.wait_ge(a1_ready, p * 2 + 4)
                dve.wait_ge(reps_ready, ops(p, idx))
                b = SLOTS[idx][0]
                if idx < 2:
                    left = a1[:, q, idx].rearrange("p (a n) -> p a n", a=1).to_broadcast([128, 2, N])
                    nc.vector.tensor_tensor(z1a[:, idx], ring[:, b:b + 2], left, ALU.mult).then_inc(z_ready, 1)
                else:
                    nc.vector.tensor_tensor(z1b[:], ring[:, b:b + 2], a1[:, q], ALU.mult).then_inc(z_ready, 1)

            def layer2(p, i, s, q):
                if i == 0 and s == 0:
                    dve.wait_ge(b_ready, p * B_COPIES + B_COPIES)
                if s == 0 and not (isinstance(p, int) and p == 0):
                    dve.wait_ge(l2_done, p * I2 + (i + 1 - I2))
                idx = L1_OPS + 2 * i + s
                dve.wait_ge(reps_ready, ops(p, idx))
                b = SLOTS[idx][0]
                x0 = ring[:, b:b + 1].to_broadcast([128, J2, N])
                nc.vector.tensor_tensor(z2[:, i, s], x0, bx[:, q, s], ALU.mult).then_inc(z_ready, 1)

            def sum_x1(p):
                dve.wait_ge(b_copied, p + 1)
                at = s1[:, p] if isinstance(p, int) else s1[:, bass.ds(p, 1)].rearrange("p a b -> p (a b)")
                nc.vector.reduce_sum(at, x1_ps[:].rearrange("p (d b) -> p b d", b=HB), AX.X).then_inc(s1_ready, 1)

            def period(p, q, last=False):
                if not last:
                    for idx in range(L1_OPS):
                        layer1(p, idx, 1 - q)
                for i in range(I2):
                    for s in range(2):
                        layer2(p, i, s, q)
                    if i == 0 and not last:
                        sum_x1(p + 1)

            dve.wait_ge(w_in, 16 * 13)
            for q in range(2 * GP):
                last_col = nc.vector.tensor_copy(bd[:, q, F, :], mask_sb[:])
            last_col.then_inc(sum_cols, 1)
            dve.wait_ge(w0_in, 32)
            nc.vector.tensor_tensor(w0_sb[:], w0a_sb[:], w0b_sb[:], ALU.add).then_inc(w0_ready, 1)
            dve.wait_ge(rows_landed, 16 * F)
            split(nc.vector, dve, emb[:, 0].rearrange("p f d -> p d f"), 0)
            dve.wait_ge(aux6_full, 1)
            for dst, src in x0t_pieces(0, 1, ps6):
                cp = nc.vector.tensor_copy(dst, src)
            cp.then_inc(x0t_half, 1)
            dve.wait_ge(x0t_half, 1)
            dve.sem_inc(aux6_free, 1)
            dve.sem_inc(x0t_ready, 1)

            def a1_copy(q):
                dve.wait_ge(aux6_full, 2 + q)
                nc.vector.tensor_copy(a1[:, q, 1], ps6[:]).then_inc(aux6_free, 1)
                dve.wait_ge(aux6_free, 2 + q)
                dve.sem_inc(a1_ready, 1)

            a1_copy(0)
            for idx in range(L1_OPS):
                layer1(-1, idx, 0)
            a1_copy(1)
            sum_x1(0)
            period(0, 0)
            with dve.Fori(0, LAST) as t:
                period(t * 2 + 1, 1)
                period(t * 2 + 2, 0)
            period(PAIRS - 1, 1, last=True)

            for s in range(2):
                nc.vector.tensor_copy(in_a[0:H, :, s, :], s1[s * H:(s + 1) * H])
            dve.wait_ge(g_ready, 2 * PAIRS)
            for s in range(2):
                cp = nc.vector.tensor_copy(in_a[H:2 * H, :, s, :], g_sb[s * H:(s + 1) * H, F])
            cp.then_inc(in_ready_v, 1)
            for s, bank in enumerate((x1_ps, x2_ps)):
                dve.wait_ge(in_ready_a, s + 1)
                z3 = in_b[0:H, :, s, :]
                nc.vector.tensor_tensor(z3, bank[H:2 * H, 0:PAIRS * HB].rearrange("p (a b) -> p a b", b=HB), z3,
                                        ALU.add).then_inc(z3_ready, 1)
            for q in range(1, Q1, 2):
                dve.wait_ge(h1_done, q + 1)
                nc.vector.tensor_scalar(h1[:, q], ring[:, q], bt1_sb[:, q:q + 1], 0.0,
                                        ALU.add, ALU.max).then_inc(h1_ready_v, 1)
            dve.wait_ge(h2_done, 2)
            nc.vector.tensor_scalar(h2[:, 1], x2_ps[:], bt2_sb[:, 1:2], 0.0, ALU.add, ALU.max)\
                .then_inc(h2_ready_v, 1)
            dve.wait_ge(y_done, 1)
            nc.vector.tensor_copy(y_sb[:], ps6[0:1, :]).then_inc(y_ready, 1)

        @block.tensor
        def _(pe):
            def cols(p, s):
                return x0t[:, p * (2 * N) + s * N:p * (2 * N) + (s + 1) * N] if isinstance(p, int) else \
                    x0t[:, bass.ds(p * (2 * N) + s * N, N)]

            def select(dst, sel, p, s):
                return nc.tensor.matmul(dst, sel, cols(p, s), start=True, stop=True)

            def reps(p, idx):
                free = slot_free(p, idx)
                if free is not None:
                    pe.wait_ge(z_ready, free)
                if idx < 2:
                    todo = [(sel_b1_sb[:, c], idx) for c in range(2)]
                elif idx == 2:
                    todo = [(sel_b1_sb[:, 2], s) for s in range(2)]
                else:
                    i, s = divmod(idx - L1_OPS, 2)
                    todo = [(sel_x0_sb[:, i], s)]
                for b, (sel, s) in zip(SLOTS[idx], todo):
                    mm = select(ring[:, b], sel, p + 1 if idx < L1_OPS else p, s)
                mm.then_inc(reps_ready, 1)

            def halves(acc, w, z, first, final):
                for s in range(2):
                    mm = nc.tensor.matmul(acc[s * H:(s + 1) * H, :], w, z(s), start=first, stop=final)
                return mm

            def main1(p, c):
                if c == 0:
                    pe.wait_ge(z_ready, ops(p, 1))
                    if not (isinstance(p, int) and p == -1):
                        pe.wait_ge(s1_ready, p + 1)
                if c == 2:
                    pe.wait_ge(z_ready, ops(p, 2))
                mm = halves(x1_ps, w0_sb[:, c], lambda s: z1b[:, s] if c == 2 else z1a[:, s, c], c == 0, c == 2)
                if c == 2:
                    mm.then_inc(x1_done, 1)

            def main2(p, i, j):
                if j == 0:
                    pe.wait_ge(z_ready, ops(p, L1_OPS + 2 * i + 1))
                    if i == 0 and not (isinstance(p, int) and p == 0):
                        pe.wait_ge(x2_copied, p * 1)
                mm = halves(x2_ps, w1_sb[:, i, j], lambda s: z2[:, i, s, j],
                            (i, j) == (0, 0), (i, j) == (I2 - 1, J2 - 1))
                if j == J2 - 1:
                    mm.then_inc(l2_done, 1)

            def transposes(tiles, part, count):
                bank, free = ((ps7, aux7_free), (ps6, aux6_free))[part]
                pe.wait_ge(parts_ready, tiles)
                if not (isinstance(count, int) and count == 1):
                    pe.wait_ge(free, count - 1)
                for d in range(8):
                    tp = nc.tensor.transpose(bank[:].bitcast(bf16)[0:XR, d * 128:(d + 1) * 128],
                                             parts[:, 8 * part + d].rearrange("p a f -> p (a f)"), eye_b_sb[:])
                tp.then_inc((aux7_full, aux6_full)[part], 1)

            def left_factor(p, s, count, parts_in, bank=7):
                bank, full, free = (ps7, aux7_full, aux7_free) if bank == 7 else (ps6, aux6_full, aux6_free)
                pe.wait_ge(x0t_ready, parts_in)
                pe.wait_ge(free, count - 1)
                select(bank[:], sel_a1_sb[:], p, s).then_inc(full, 1)

            def x0_by_column(p, count):
                pe.wait_ge(aux6_free, count - 1)
                for s in range(2):
                    for g in range(GP):
                        by_group = x0t[:].rearrange("r (m g) -> r g m", g=GP)[:, g]
                        at = p * (2 * 128) + s * 128
                        c = by_group[:, at:at + 128] if isinstance(p, int) else by_group[:, bass.ds(at, 128)]
                        q = s * GP + g
                        mm = nc.tensor.matmul(ps6[:, q * F:(q + 1) * F], c, sel_n_sb[:], start=True, stop=True)
                mm.then_inc(aux6_full, 1)

            def x2_by_column(p, count):
                pe.wait_ge(x2_copied, p + 1)
                pe.wait_ge(aux6_free, count - 1)
                for g in range(GP):
                    c = x2_sb[:].rearrange("r (m g) -> r g m", g=GP)[:, g]
                    tp = nc.tensor.transpose(ps6[:, g * 128:(g + 1) * 128], c, eye_f_sb[:])
                tp.then_inc(aux6_full, 1)

            def outer_sums(p, count6, count7):
                pe.wait_ge(x2t_ready, p + 1)
                pe.wait_ge(bd_ready, p + 1)
                for g in range(GP):
                    if g == 0:
                        pe.wait_ge(aux7_free, count7 - 1)
                    if g == 2:
                        pe.wait_ge(aux6_free, count6 - 1)
                    bank = (ps7, ps6)[g // 2]
                    at = (g % 2) * GC
                    for s in range(2):
                        mm = nc.tensor.matmul(bank[s * H:(s + 1) * H, at:at + GC], x2t[:, g, s * H:(s + 1) * H],
                                              bd[:, s * GP + g].rearrange("p f b -> p (f b)"),
                                              start=True, stop=True)
                    if g == 1:
                        mm.then_inc(aux7_full, 1)
                    if g == 3:
                        mm.then_inc(aux6_full, 1)

            def early(p, t, x, last=False):
                if not last:
                    reps(p, 1)
                main2(p - 1, 1, 2)
                if not last:
                    reps(p, 2)
                main2(p - 1, 1, 3)
                reps(p, 3)
                reps(p, 4)
                if not last:
                    main1(p, 0)
                reps(p, 5)
                reps(p, 6)
                if not last:
                    main1(p, 1)
                    main1(p, 2)
                main2(p - 1, 2, 0)
                main2(p - 1, 2, 1)
                reps(p, 7)
                main2(p - 1, 2, 2)
                main2(p - 1, 2, 3)
                reps(p, 8)
                x2_by_column(p - 1, aux6(t, "X2T_" + x))
                main2(p, 0, 0)
                outer_sums(p - 1, aux6(t, "G1_" + x), aux7(t, "G0_" + x))

            def late(p, t, x, last=False):
                main2(p, 0, 1)
                if x == "e" and not last:
                    transposes(t + 2, 0, aux7(t, "T0"))
                    transposes(t + 2, 1, aux6(t, "T1"))
                main2(p, 0, 2)
                main2(p, 0, 3)
                if not last:
                    left_factor(p + 2, 0, aux7(t, "A1_%s0" % x), t * 2 + 4)
                    reps(p + 1, 0)
                main2(p, 1, 0)
                if not last:
                    left_factor(p + 2, 1, aux7(t, "A1_%s1" % x), t * 2 + 4)
                x0_by_column(p, aux6(t, "X0n_" + x))
                main2(p, 1, 1)

            pe.wait_ge(consts_in, 16 * 4)
            pe.wait_ge(gathers_issued, 1)
            for _ in range(WARM):
                nc.tensor.matmul(x2_ps[:, 0:128], eye_b_sb[:], eye_b_sb[:], start=True, stop=True)
            transposes(1, 0, 1)
            transposes(1, 1, 1)
            left_factor(0, 0, 2, 2)
            left_factor(0, 1, 2, 2, bank=6)
            for idx in range(L1_OPS):
                reps(-1, idx)
            pe.wait_ge(w0_ready, 1)
            for c in range(C1):
                main1(-1, c)
            left_factor(1, 0, 3, 2)
            left_factor(1, 1, 3, 2, bank=6)
            for idx in range(5):
                reps(0, idx)
            main1(0, 0)
            reps(0, 5)
            reps(0, 6)
            main1(0, 1)
            main1(0, 2)
            reps(0, 7)
            reps(0, 8)
            pe.wait_ge(w_in, 16 * 13)
            main2(0, 0, 0)
            with pe.Fori(0, LAST) as t:
                late(t * 2, t, "e")
                early(t * 2 + 1, t, "e")
                late(t * 2 + 1, t, "o")
                early(t * 2 + 2, t, "o")
            p = PAIRS - 1
            late(p - 1, LAST, "e", last=True)
            early(p, LAST, "e", last=True)
            late(p, LAST, "o", last=True)
            main2(p, 1, 2)
            main2(p, 1, 3)
            for j in range(J2):
                main2(p, 2, j)
            x2_by_column(p, aux6(LAST, "X2T_o"))
            outer_sums(p, aux6(LAST, "G1_o"), aux7(LAST, "G0_o"))

            pe.wait_ge(g_ready, 2 * PAIRS)
            for f in range(0, F, 2):
                for odd in range(2):
                    for s, bank in enumerate((x1_ps, x2_ps)):
                        mm = nc.tensor.matmul(bank[odd * H:(odd + 1) * H, 0:PAIRS * HB],
                                              w2_sb[s * H:(s + 1) * H, f + odd],
                                              g_sb[s * H:(s + 1) * H, f + odd].rearrange("p a b -> p (a b)"),
                                              start=(f == 0), stop=(f == F - 2))
            mm.then_inc(z3_done, 1)

            pe.wait_ge(in_ready_v, 1)
            for q in range(Q1):
                nc.tensor.matmul(ring[:, q], wt1a_sb[:, q * 128:(q + 1) * 128],
                                 in_a[:].rearrange("p a s b -> p (a s b)"), start=True, stop=False)
            pe.wait_ge(z3_ready, 2)
            for q in range(Q1):
                nc.tensor.matmul(ring[:, q], wt1b_sb[:, q * 128:(q + 1) * 128],
                                 in_b[:].rearrange("p a s b -> p (a s b)"), start=False, stop=True)\
                    .then_inc(h1_done, 1)
            for m, bank in enumerate((x1_ps, x2_ps)):
                for q in range(Q1):
                    if m == 0:
                        pe.wait_ge((h1_ready_a, h1_ready_v)[q % 2], q // 2 + 1)
                    mm = nc.tensor.matmul(bank[:], wt2_sb[:, q, m * 128:(m + 1) * 128], h1[:, q],
                                          start=(q == 0), stop=(q == Q1 - 1))
                mm.then_inc(h2_done, 1)
            for m in range(Q2):
                pe.wait_ge((h2_ready_a, h2_ready_v)[m], 1)
                mm = nc.tensor.matmul(ps6[0:1, :], wt3_sb[:, m:m + 1], h2[:, m], start=(m == 0), stop=(m == Q2 - 1))
            mm.then_inc(y_done, 1)

        @block.scalar
        def _(act):
            def copy(dst, src):
                return nc.scalar.activation(dst, src, ACT.Copy)

            def x0t_copy(t, part, count):
                bank, full, free = ((ps7, aux7_full, aux7_free), (ps6, aux6_full, aux6_free))[part]
                act.wait_ge(full, count)
                for dst, src in x0t_pieces(t, part, bank):
                    cp = copy(dst, src)
                cp.then_inc(free, 1)
                act.wait_ge(free, count)
                act.sem_inc(x0t_ready, 1)

            def a1_copy(parity, s, count):
                act.wait_ge(aux7_full, count)
                copy(a1[:, parity, s], ps7[:]).then_inc(aux7_free, 1)
                act.wait_ge(aux7_free, count)
                act.sem_inc(a1_ready, 1)

            def b_copy(p):
                act.wait_ge(x1_done, p + 1)
                if not (isinstance(p, int) and p == 0):
                    act.wait_ge(b_ready, p * B_COPIES)
                for s in range(2):
                    for h in range(QH):
                        at = s * H + h * 32
                        cp = copy(x1q[:, s, h], x1_ps[at:at + 32, :])
                cp.then_inc(b_copied, 1)

            def bd_build(t, p, name):
                act.wait_ge(aux6_full, aux6(t, name))
                for b in range(GB):
                    cp = nc.scalar.activation(bd[:, :, 0:F, b], ps6[:, 0:2 * GP * F].rearrange("p (q f) -> p q f", f=F),
                                              ACT.Copy, scale=mask_sb[:, b:b + 1])
                cp.then_inc(aux6_free, 1)
                act.wait_ge(aux6_free, aux6(t, name))
                act.sem_inc(bd_ready, 1)

            def x2_copy(p):
                act.wait_ge(l2_done, p * I2 + I2)
                copy(x2_sb[:], x2_ps[:]).then_inc(x2_copied, 1)

            def x2t_copy(t, name):
                act.wait_ge(aux6_full, aux6(t, name))
                copy(x2t[:].rearrange("p g c -> p (g c)"), ps6[:]).then_inc(aux6_free, 1)
                act.wait_ge(aux6_free, aux6(t, name))
                act.sem_inc(x2t_ready, 1)

            def g_copy(t, p, odd):
                x = "eo"[odd]
                for part, (bank, full, free, count) in enumerate((
                        (ps7, aux7_full, aux7_free, aux7(t, "G0_" + x)), (ps6, aux6_full, aux6_free, aux6(t, "G1_" + x)))):
                    act.wait_ge(full, count)
                    src = bank[:, 0:2 * GC].rearrange("p (g f b) -> p f b g", g=2, b=GB)
                    dst = g_sb[:].rearrange("p f a (b g) -> p f (a b) g", g=GP)
                    dst = dst[:, :, p * GB:(p + 1) * GB] if isinstance(p, int) else dst[:, :, bass.ds(p * GB, GB)]
                    dst = dst[:, :, :, 2 * part:2 * part + 2]
                    copy(dst, src).then_inc(free, 1)
                    act.wait_ge(free, count)
                    act.sem_inc(g_ready, 1)

            def early(p, t, odd, last=False):
                if not last:
                    b_copy(p + 1)
                x2_copy(p - 1)
                x2t_copy(t, "X2T_" + "eo"[odd])
                g_copy(t, p - 1, odd)

            def late(p, t, odd, last=False):
                x = "eo"[odd]
                if not last:
                    if not odd:
                        x0t_copy(t + 1, 0, aux7(t, "T0"))
                        x0t_copy(t + 1, 1, aux6(t, "T1"))
                    for s in range(2):
                        a1_copy(odd, s, aux7(t, "A1_%s%d" % (x, s)))
                bd_build(t, p, "X0n_" + x)

            x0t_copy(0, 0, 1)
            a1_copy(0, 0, 2)
            b_copy(0)
            a1_copy(1, 0, 3)
            b_copy(1)
            act.wait_ge(w_in, 16 * 13)
            act.wait_ge(sum_cols, 1)
            with act.Fori(0, LAST) as t:
                late(t * 2, t, 0)
                early(t * 2 + 1, t, 0)
                late(t * 2 + 1, t, 1)
                early(t * 2 + 2, t, 1)
            late(PAIRS - 2, LAST, 0, True)
            early(PAIRS - 1, LAST, 0, last=True)
            late(PAIRS - 1, LAST, 1, True)
            x2_copy(PAIRS - 1)
            x2t_copy(LAST, "X2T_o")
            g_copy(LAST, PAIRS - 1, 1)

            act.wait_ge(z3_done, 1)
            for s, bank in enumerate((x1_ps, x2_ps)):
                copy(in_b[0:H, :, s, :], bank[0:H, 0:PAIRS * HB].rearrange("p (a b) -> p a b", b=HB))\
                    .then_inc(in_ready_a, 1)
            for q in range(0, Q1, 2):
                act.wait_ge(h1_done, q + 1)
                nc.scalar.activation(h1[:, q], ring[:, q], ACT.Relu, bias=bt1_sb[:, q:q + 1])\
                    .then_inc(h1_ready_a, 1)
            act.wait_ge(h2_done, 1)
            nc.scalar.activation(h2[:, 0], x1_ps[:], ACT.Relu, bias=bt2_sb[:, 0:1]).then_inc(h2_ready_a, 1)


def _field_pairs():
    rows = []
    for c in range(C1):
        for p in range(128):
            k, f = c * KC + p // F, p % F
            ok = p < KC * F and (k < KD - 1 or (k == KD - 1 and f < F // 2))
            rows.append((f, (f + k) % F) if ok else None)
    return rows


def kernel(**inputs):
    import ml_dtypes
    import concourse.bacc as _bacc
    from concourse.bass_utils import run_bass_kernel_spmd as _run

    x = {k: np.asarray(v) for k, v in inputs.items()}
    bf = ml_dtypes.bfloat16
    w0 = x["L0_rec_W0"]
    w0a = np.zeros((C1 * 128, H), w0.dtype)
    w0b = np.zeros((C1 * 128, H), w0.dtype)
    sel_b1 = np.zeros((F, C1, 128), bf)
    for r, fh in enumerate(_field_pairs()):
        if fh is None:
            continue
        f, h = fh
        w0a[r] = w0[f * F + h]
        if f != h:
            w0b[r] = w0[h * F + f]
        sel_b1[h, r // 128, r % 128] = 1
    by_block = lambda w: np.ascontiguousarray(w.reshape(C1, 128, H).transpose(1, 0, 2))
    w1 = x["L0_rec_W1"].reshape(I2, U2, J2, V2, H).transpose(1, 3, 0, 2, 4).reshape(128, I2, J2, H)
    w2 = x["L0_rec_W2"].reshape(F, H, H).transpose(1, 0, 2)
    sel_a1 = np.zeros((F, 128), bf)
    sel_x0 = np.zeros((F, I2, 128), bf)
    for p in range(KC * F):
        sel_a1[p % F, p] = 1
    for i in range(I2):
        for p in range(128):
            sel_x0[U2 * i + p // V2, i, p] = 1
    three = lambda a: np.concatenate([a] * PARTS, axis=0)
    mask = np.zeros((128, GB), np.float32)
    for p in range(128):
        mask[p, p % GB] = 1
    arrays = {
        "ids": x["ids"].reshape(TILES, 128, F).transpose(1, 0, 2),
        "dense_t": x["dense_ctx"].T,
        "w0a": by_block(w0a), "w0b": by_block(w0b), "w1": w1, "w2": w2,
        "wt1": x["W_top1"], "bt1": x["b_top1"].reshape(Q1, 128).T,
        "wt2": x["W_top2"].reshape(Q1, 128, M2).transpose(1, 0, 2), "bt2": x["b_top2"].reshape(Q2, 128).T,
        "wt3": x["W_top3"].reshape(Q2, 128).T,
        "sel_a1": three(sel_a1), "sel_b1": three(sel_b1), "sel_x0": three(sel_x0),
        "sel_n": three(np.eye(F, dtype=bf)), "eye_f": np.eye(128, dtype=np.float32),
        "eye_b": np.eye(128, dtype=bf), "mask": mask,
    }
    for f in range(F):
        arrays[f"tbl_{f}"] = x[f"tbl_{f}"]
    arrays = {k: np.ascontiguousarray(v) for k, v in arrays.items()}

    nc = _bacc.Bacc("TRN2", target_bir_lowering=False, num_devices=1)
    aps = {k: nc.dram_tensor(k, v.shape, mybir.dt.from_np(v.dtype), kind="ExternalInput").ap()
           for k, v in arrays.items()}
    out = nc.dram_tensor("y", (B, 1), mybir.dt.float32, kind="ExternalOutput").ap()
    tables = [aps.pop(f"tbl_{f}") for f in range(F)]
    dlrm_tower(nc, tables=tables, out=out.rearrange("b o -> o b"), **aps)
    r = _run(nc, [arrays], core_ids=[0])
    return r.results[0]["y"]
```

```python
from contextlib import ExitStack

import numpy as np

import concourse.bass as bass
from concourse import mybir

B, F, D = 512, 24, 16
H = 64
PARTS = 3
XR = PARTS * F
TILES = B // 128
PAIRS = 2 * TILES
HB = 32
N = HB * D
LAST = TILES - 1
KD = F // 2 + 1
KC = 5
C1 = -(-KD // KC)
U2 = 8
V2 = 16
I2, J2 = F // U2, H // V2
JH = J2 // 2
GB = 8
GP = HB // GB
FH = F // 2
GC = (FH + 1) * GB
M1, M2 = 512, 256
Q1, Q2 = M1 // 128, M2 // 128
HEAD = 20


def dlrm_tower(nc, ids, tables, dense_t, w0a, w0b, w1, w2, wt1, bt1, wt2, bt2, wt3,
               sel_a1, sel_b1, sel_n, eye_f, eye_b, mask, x0_rows, x1_rows, out):
    f32, bf16, i32 = mybir.dt.float32, mybir.dt.bfloat16, mybir.dt.int32
    ALU, ACT, AX = mybir.AluOpType, mybir.ActivationFunctionType, mybir.AxisListType

    L1_OPS, OPS = 3, 3 + 2 * I2
    SLOTS = [(0, 1), (2, 3), (0, 1)]

    def ops(p, idx):
        if isinstance(p, int) and p == -1:
            return idx + 1
        n = p * OPS + (idx + L1_OPS + 1)
        return n - L1_OPS if isinstance(p, int) and p == PAIRS - 1 else n

    def slot_free(p, idx):
        if idx == 2:
            return ops(p, 0)
        if isinstance(p, int) and p == -1:
            return None
        return ops(p - 1, (2, 1)[idx])

    def reps_up_to(p, idx):
        return p * L1_OPS + (idx + L1_OPS + 1)

    AUX6 = ["T1", "A1_e1", "X0n_e", "X2T_e", "G1_e", "A1_o1", "X0n_o", "X2T_o", "G1_o"]
    AUX7 = ["T0", "A1_e0", "G0_e", "A1_o0", "G0_o"]
    PRE6, PRE7 = 3, 3

    def aux6(t, name):
        order = [x for x in AUX6 if x[0] in "XG"] if isinstance(t, int) else AUX6
        return t * len(AUX6) + (PRE6 + order.index(name) + 1)

    def aux7(t, name):
        order = [x for x in AUX7 if x[0] == "G"] if isinstance(t, int) else AUX7
        return t * len(AUX7) + (PRE7 + order.index(name) + 1)

    with ExitStack() as ctx:
        def sb(name, shape, dt=f32):
            return ctx.enter_context(nc.sbuf_tensor(name, shape, dt))

        def psum(name, shape):
            return ctx.enter_context(nc.psum_tensor(name, shape, f32))

        def sem(name):
            return ctx.enter_context(nc.semaphore(name))

        ids_sb = sb("ids_sb", [128, TILES, F], i32)
        w0a_sb = sb("w0a_sb", [128, C1, H])
        w0b_sb = sb("w0b_sb", [128, C1, H])
        w0_sb = sb("w0_sb", [128, C1, H])
        w1_sb = sb("w1_sb", [128, I2, J2, H])
        w2_sb = sb("w2_sb", [128, FH, H])
        wt1a_sb = sb("wt1a_sb", [128, M1])
        wt1b_sb = sb("wt1b_sb", [H + D, M1])
        wt2_sb = sb("wt2_sb", [128, Q1, M2])
        wt3_sb = sb("wt3_sb", [128, Q2])
        bt1_sb = sb("bt1_sb", [128, Q1])
        bt2_sb = sb("bt2_sb", [128, Q2])
        sel_a1_sb = sb("sel_a1_sb", [XR, 128], bf16)
        sel_b1_sb = sb("sel_b1_sb", [XR, C1, 128], bf16)
        sel_n_sb = sb("sel_n_sb", [XR, F], bf16)
        eye_f_sb = sb("eye_f_sb", [128, 128])
        eye_b_sb = sb("eye_b_sb", [128, 128], bf16)
        mask_sb = sb("mask_sb", [128, GB])
        emb = sb("emb", [128, TILES, F, D])
        rest = sb("rest", [128, D, F])
        parts = sb("parts", [128, D, PARTS, F], bf16)
        x0t = sb("x0t", [XR, PAIRS * 2 * N], bf16)
        a1 = sb("a1", [128, 2, 2, N])
        z1a = sb("z1a", [128, 2, 2, N])
        z1b = sb("z1b", [128, 2, N])
        x1_sb = sb("x1_sb", [128, N])
        ax = sb("ax", [128, I2, 2, N])
        bx = sb("bx", [128, 2, 2, J2, N])
        z2 = sb("z2", [128, I2, 2, J2, N])
        x2_sb = sb("x2_sb", [128, N])
        x2t = sb("x2t", [128, GP, 128])
        bd = sb("bd", [128, 2 * GP, 2, FH + 1, GB])
        g_sb = sb("g_sb", [128, 2, FH + 1, PAIRS, HB])
        s1 = sb("s1", [128, PAIRS, HB])
        in_a = sb("in_a", [128, PAIRS, 2, HB])
        in_b = sb("in_b", [H + D, PAIRS, 2, HB])
        h1 = z2[:, 0, 0]
        h2 = z2[:, 0, 1, 0:Q2]
        y_sb = sb("y_sb", [1, B])
        ring = psum("ring", [128, 4, N])
        x1_ps = psum("x1_ps", [128, N])
        x2_ps = psum("x2_ps", [128, N])
        ps6 = psum("ps6", [128, N])
        ps7 = psum("ps7", [128, N])

        ids_in = sem("ids_in")
        consts_in = sem("consts_in")
        w0_in = sem("w0_in")
        w_in = sem("w_in")
        head_landed = sem("head_landed")
        landed = [sem("landed_%d" % t) for t in range(TILES)]
        split_step = sem("split_step")
        parts_ready = sem("parts_ready")
        w0_ready = sem("w0_ready")
        reps_ready = sem("reps_ready")
        z_ready = sem("z_ready")
        z_start = sem("z_start")
        x1_done = sem("x1_done")
        l2_done = sem("l2_done")
        s1_ready = sem("s1_ready")
        x0_stored = sem("x0_stored")
        ax_ready = [sem("ax_ready_%d" % i) for i in range(I2)]
        b_copied = sem("b_copied")
        x1_stored = sem("x1_stored_0"), sem("x1_stored_1")
        b_ready = sem("b_ready_0"), sem("b_ready_1")
        b_first = sem("b_first_0"), sem("b_first_1")
        aux6_full, aux6_free = sem("aux6_full"), sem("aux6_free")
        aux7_full, aux7_free = sem("aux7_full"), sem("aux7_free")
        x0t_ready = sem("x0t_ready")
        x0t_half = sem("x0t_half")
        a1_ready = sem("a1_ready")
        bd_ready = sem("bd_ready")
        sum_cols = sem("sum_cols")
        x2_copied = sem("x2_copied")
        x2t_ready = sem("x2t_ready")
        g_ready = sem("g_ready")
        z3_done = sem("z3_done")
        in_ready_v = sem("in_ready_v")
        z3_ready_v, z3_ready_a = sem("z3_ready_v"), sem("z3_ready_a")
        h1_done = sem("h1_done")
        h1_ready_v, h1_ready_a = sem("h1_ready_v"), sem("h1_ready_a")
        h2_done = sem("h2_done")
        h2_ready_v, h2_ready_a = sem("h2_ready_v"), sem("h2_ready_a")
        y_done = sem("y_done")
        y_ready = sem("y_ready")
        y_out = sem("y_out")

        block = ctx.enter_context(nc.Block())

        def split_views(t, first, end):
            return (emb[:, t, first:end].rearrange("p f d -> p d f"), rest[:, :, first:end],
                    *(parts[:, :, k, first:end] for k in range(PARTS)))

        def split(builder, engine, t, first, end, turn, final):
            e, left, hi, mid, lo = split_views(t, first, end)
            builder.tensor_copy(hi, e).then_inc(split_step, 1)
            engine.wait_ge(split_step, 3 * turn + 1)
            builder.tensor_tensor(left, e, hi, ALU.subtract).then_inc(split_step, 1)
            engine.wait_ge(split_step, 3 * turn + 2)
            builder.tensor_copy(mid, left).then_inc(split_step, 1)
            engine.wait_ge(split_step, 3 * turn + 3)
            step = builder.tensor_tensor(lo, left, mid, ALU.subtract)
            if final:
                step.then_inc(parts_ready, 1)

        def x0t_pieces(t, part, bank):
            at = x0t[:, t * 4 * N:(t + 1) * 4 * N] if isinstance(t, int) else x0t[:, bass.ds(t * (4 * N), 4 * N)]
            dst = at.rearrange("r (q d b) -> r q d b", q=4, b=HB)[:, :, 8 * part:8 * part + 8]
            src = bank[:].bitcast(bf16)[0:XR, :].rearrange("r (d q b) -> r q d b", q=4, b=HB)
            return [(dst[:, q], src[:, q]) for q in range(4)]

        @block.sync
        def _(sp):
            sp.dma_start(ids_sb[:], ids).then_inc(ids_in, 16)
            for dst, src in ((eye_b_sb, eye_b), (sel_a1_sb, sel_a1), (sel_b1_sb, sel_b1)):
                sp.dma_start(dst[:], src).then_inc(consts_in, 16)
            for dst, src in ((w0a_sb, w0a), (w0b_sb, w0b)):
                sp.dma_start(dst[:], src).then_inc(w0_in, 16)
            for dst, src in ((w1_sb[:], w1), (sel_n_sb[:], sel_n), (mask_sb[:], mask), (eye_f_sb[:], eye_f),
                             (w2_sb[:], w2),
                             (wt1a_sb[:], wt1[0:128]), (wt1b_sb[:], wt1[128:2 * H + H + D]),
                             (wt2_sb[:], wt2), (wt3_sb[:], wt3), (bt1_sb[:], bt1), (bt2_sb[:], bt2),
                             (in_b[H:H + D].rearrange("p a s b -> p (a s b)"), dense_t)):
                sp.dma_start(dst, src).then_inc(w_in, 16)

            def x0_store(p):
                sp.wait_ge(a1_ready, 2 * (p + 1))
                sp.dma_start(x0_rows[p].rearrange("f s n -> f (s n)"),
                             a1[0:F, p % 2].rearrange("f s n -> f (s n)")).then_inc(x0_stored, 16)

            def ax_load(p, i):
                if p:
                    sp.wait_ge(z_ready, ops(p - 1, L1_OPS + 2 * i + 1))
                sp.wait_ge(x0_stored, 16 * (p + 1))
                src = x0_rows[p, U2 * i:U2 * (i + 1)].rearrange("u (a s) n -> u a (s n)", a=1)
                sp.dma_start(ax[:, i].rearrange("p s n -> p (s n)"), src.to_broadcast([U2, V2, 2 * N]))\
                    .then_inc(ax_ready[i], 16)

            x0_store(0)
            for p in range(PAIRS):
                for i in range(I2 if p == 0 else 1):
                    ax_load(p, i)
                if p >= 2:
                    sp.wait_ge(z_ready, ops(p - 2, OPS - 1))
                sp.wait_ge(b_copied, p + 1)
                for s in range(2):
                    sp.dma_start(x1_rows[p, s].rearrange("v j n -> j v n"), x1_sb[s * H:(s + 1) * H])\
                        .then_inc(x1_stored[s], 16)
                for landed_in, js in ([(b_first, slice(0, JH)), (b_ready, slice(JH, J2))] if p == 0 else
                                      [(b_ready, slice(0, J2))]):
                    for s in range(2):
                        sp.wait_ge(x1_stored[s], 16 * (p + 1))
                        if p:
                            sp.wait_ge(b_ready[s], 16 * p)
                        src = x1_rows[p, s:s + 1, :, js].rearrange("a v j n -> a v (j n)")
                        sp.dma_start(bx[:, p % 2, s, js], src.to_broadcast([U2, V2, src.shape[2]]))\
                            .then_inc(landed_in[s], 16)
                for i in range(1, I2 if p else 1):
                    ax_load(p, i)
                if p + 1 < PAIRS:
                    x0_store(p + 1)
            sp.wait_ge(y_ready, 2)
            sp.dma_start(out, y_sb[:]).then_inc(y_out, 16)
            sp.wait_ge(y_out, 16)

        @block.gpsimd
        def _(pool):
            pool.wait_ge(ids_in, 16)
            for t in range(TILES):
                for f in range(F):
                    nc.gpsimd.indirect_dma_start(
                        out=emb[:, t, f, :], out_offset=None, in_=tables[f][:, :],
                        in_offset=bass.IndirectOffsetOnAxis(ap=ids_sb[:, t, f:f + 1], axis=0),
                    ).then_inc(head_landed if t == 0 and f < HEAD else landed[t], 16)
                if t == 1:
                    e, left, hi, mid, lo = split_views(t, 0, F)
                    pool.wait_ge(split_step, 3 * (t + 1) + 1)
                    nc.gpsimd.tensor_tensor(left, e, hi, ALU.subtract).then_inc(split_step, 1)
                    pool.wait_ge(split_step, 3 * (t + 1) + 3)
                    nc.gpsimd.tensor_tensor(lo, left, mid, ALU.subtract).then_inc(parts_ready, 1)
                if t > 1:
                    pool.wait_ge(landed[t], 16 * F)
                    pool.wait_ge(x0t_ready, 2 * t)
                    split(nc.gpsimd, pool, t, 0, F, t + 1, True)

        @block.vector
        def _(dve):
            def layer1(p, idx, q):
                if idx == 0:
                    if not (isinstance(p, int) and p == -1):
                        dve.wait_ge(x1_done, p + 1)
                    dve.wait_ge(a1_ready, p * 2 + 4)
                dve.wait_ge(reps_ready, reps_up_to(p, idx))
                b = SLOTS[idx][0]
                if idx < 2:
                    left = a1[:, q, idx].rearrange("p (a n) -> p a n", a=1).to_broadcast([128, 2, N])
                    nc.vector.tensor_tensor(z1a[:, idx], ring[:, b:b + 2], left, ALU.mult).then_inc(z_ready, 1)
                else:
                    nc.vector.tensor_tensor(z1b[:], ring[:, b:b + 2], a1[:, q], ALU.mult).then_inc(z_ready, 1)

            def layer2(p, i, s, q):
                if i == 0:
                    dve.wait_ge(b_ready[s], p * 16 + 16)
                if s == 0:
                    if not (isinstance(p, int) and p == 0):
                        dve.wait_ge(l2_done, p * I2 + (i + 1 - I2))
                    dve.wait_ge(ax_ready[i], p * 16 + 16)
                x0 = ax[:, i, s:s + 1].to_broadcast([128, J2, N])
                nc.vector.tensor_tensor(z2[:, i, s], x0, bx[:, q, s], ALU.mult).then_inc(z_ready, 1)

            def layer2_start():
                dve.wait_ge(ax_ready[0], 16)
                for landed_in, done, js in ((b_first, z_start, slice(0, JH)), (b_ready, z_ready, slice(JH, J2))):
                    for s in range(2):
                        dve.wait_ge(landed_in[s], 16)
                        x0 = ax[:, 0, s:s + 1].to_broadcast([128, JH, N])
                        nc.vector.tensor_tensor(z2[:, 0, s, js], x0, bx[:, 0, s, js], ALU.mult).then_inc(done, 1)

            def sum_x1(p):
                dve.wait_ge(b_copied, p + 1)
                at = s1[:, p] if isinstance(p, int) else s1[:, bass.ds(p, 1)].rearrange("p a b -> p (a b)")
                nc.vector.reduce_sum(at, x1_ps[:].rearrange("p (d b) -> p b d", b=HB), AX.X).then_inc(s1_ready, 1)

            def period(p, q, last=False):
                if not last:
                    for idx in range(L1_OPS):
                        layer1(p, idx, 1 - q)
                for i in range(I2):
                    if i == 0 and isinstance(p, int) and p == 0:
                        layer2_start()
                    else:
                        for s in range(2):
                            layer2(p, i, s, q)
                    if i == 1 and not last:
                        sum_x1(p + 1)

            def a1_copy(parity, count):
                dve.wait_ge(aux6_full, count)
                nc.vector.tensor_copy(a1[:, parity, 1], ps6[:]).then_inc(aux6_free, 1)
                dve.wait_ge(aux6_free, count)
                dve.sem_inc(a1_ready, 1)

            dve.wait_ge(w_in, 16 * 12)
            nc.vector.tensor_copy(bd[:, :, :, FH, :].rearrange("p q c b -> p (q c) b"),
                                  mask_sb[:].rearrange("p (a b) -> p a b", a=1).to_broadcast([128, 4 * GP, GB]))\
                .then_inc(sum_cols, 1)
            dve.wait_ge(w0_in, 32)
            nc.vector.tensor_tensor(w0_sb[:], w0a_sb[:], w0b_sb[:], ALU.add).then_inc(w0_ready, 1)
            dve.wait_ge(head_landed, 16 * HEAD)
            split(nc.vector, dve, 0, 0, HEAD, 0, False)
            dve.wait_ge(landed[0], 16 * (F - HEAD))
            split(nc.vector, dve, 0, HEAD, F, 1, True)
            dve.wait_ge(aux6_full, 1)
            for dst, src in x0t_pieces(0, 1, ps6):
                cp = nc.vector.tensor_copy(dst, src)
            cp.then_inc(x0t_half, 1)
            dve.wait_ge(x0t_half, 1)
            dve.sem_inc(aux6_free, 1)
            dve.sem_inc(x0t_ready, 1)

            a1_copy(0, 2)
            for idx in range(L1_OPS):
                layer1(-1, idx, 0)
            a1_copy(1, 3)
            sum_x1(0)
            period(0, 0)
            with dve.Fori(0, LAST) as t:
                period(t * 2 + 1, 1)
                period(t * 2 + 2, 0)
            period(PAIRS - 1, 1, last=True)

            for s in range(2):
                nc.vector.tensor_copy(in_a[0:H, :, s, :], s1[s * H:(s + 1) * H])
            for first, end in ((0, PAIRS - 1), (PAIRS - 1, PAIRS)):
                dve.wait_ge(g_ready, 2 * end)
                for s in range(2):
                    cp = nc.vector.tensor_copy(in_a[H:2 * H, first:end, s, :], g_sb[H:2 * H, s, FH, first:end])
                cp.then_inc(in_ready_v, 1)
            dve.wait_ge(z3_done, 1)
            nc.vector.tensor_copy(in_b[0:H, :, 1, :],
                                  x2_ps[H:2 * H, 0:PAIRS * HB].rearrange("p (a b) -> p a b", b=HB))\
                .then_inc(z3_ready_v, 1)
            for q in range(1, Q1, 2):
                dve.wait_ge(h1_done, q + 1)
                nc.vector.tensor_scalar(h1[:, q], ring[:, q], bt1_sb[:, q:q + 1], 0.0,
                                        ALU.add, ALU.max).then_inc(h1_ready_v, 1)
            dve.wait_ge(h2_done, 2)
            for c in range(2):
                at = slice(c * B // 2, (c + 1) * B // 2)
                nc.vector.tensor_scalar(h2[:, 1, at], x2_ps[:, at], bt2_sb[:, 1:2], 0.0, ALU.add, ALU.max)\
                    .then_inc(h2_ready_v, 1)
            for c, bank in enumerate((ps6, ps7)):
                dve.wait_ge(y_done, c + 1)
                nc.vector.tensor_copy(y_sb[:, c * B // 2:(c + 1) * B // 2], bank[c * H:c * H + 1, 0:B // 2])\
                    .then_inc(y_ready, 1)

        @block.tensor
        def _(pe):
            def cols(p, s):
                return x0t[:, p * (2 * N) + s * N:p * (2 * N) + (s + 1) * N] if isinstance(p, int) else \
                    x0t[:, bass.ds(p * (2 * N) + s * N, N)]

            def select(dst, sel, p, s):
                return nc.tensor.matmul(dst, sel, cols(p, s), start=True, stop=True)

            def reps(p, idx):
                free = slot_free(p, idx)
                if free is not None:
                    pe.wait_ge(z_ready, free)
                todo = [(c, idx) for c in range(2)] if idx < 2 else [(2, s) for s in range(2)]
                for b, (c, s) in zip(SLOTS[idx], todo):
                    mm = select(ring[:, b], sel_b1_sb[:, c], p + 1, s)
                mm.then_inc(reps_ready, 1)

            def halves(acc, w, z, first, final):
                for s in range(2):
                    mm = nc.tensor.matmul(acc[s * H:(s + 1) * H, :], w, z(s), start=first, stop=final)
                return mm

            def main1(p, c):
                if c == 0:
                    pe.wait_ge(z_ready, ops(p, 1))
                    if not (isinstance(p, int) and p == -1):
                        pe.wait_ge(s1_ready, p + 1)
                if c == 2:
                    pe.wait_ge(z_ready, ops(p, 2))
                mm = halves(x1_ps, w0_sb[:, c], lambda s: z1b[:, s] if c == 2 else z1a[:, s, c], c == 0, c == 2)
                if c == 2:
                    mm.then_inc(x1_done, 1)

            def main2(p, i, j):
                if isinstance(p, int) and (p, i, j) == (0, 0, 0):
                    pe.wait_ge(z_start, 2)
                elif j == 0 or (i, j) == (0, JH):
                    pe.wait_ge(z_ready, ops(p, L1_OPS + 2 * i + 1))
                    if (i, j) == (0, 0):
                        pe.wait_ge(x2_copied, p * 1)
                mm = halves(x2_ps, w1_sb[:, i, j], lambda s: z2[:, i, s, j],
                            (i, j) == (0, 0), (i, j) == (I2 - 1, J2 - 1))
                if j == J2 - 1:
                    mm.then_inc(l2_done, 1)

            def transposes(tiles, part, count):
                bank, free = ((ps7, aux7_free), (ps6, aux6_free))[part]
                pe.wait_ge(parts_ready, tiles)
                if not (isinstance(count, int) and count == 1):
                    pe.wait_ge(free, count - 1)
                for d in range(8):
                    tp = nc.tensor.transpose(bank[:].bitcast(bf16)[0:XR, d * 128:(d + 1) * 128],
                                             parts[:, 8 * part + d].rearrange("p a f -> p (a f)"), eye_b_sb[:])
                tp.then_inc((aux7_full, aux6_full)[part], 1)

            def left_factor(p, s, count, parts_in):
                bank, full, free = ((ps7, aux7_full, aux7_free), (ps6, aux6_full, aux6_free))[s]
                pe.wait_ge(x0t_ready, parts_in)
                pe.wait_ge(free, count - 1)
                select(bank[:], sel_a1_sb[:], p, s).then_inc(full, 1)

            def x0_by_column(p, q, count):
                if q == 0:
                    pe.wait_ge(aux6_free, count - 1)
                by_group = x0t[:].rearrange("r (m g) -> r g m", g=GP)[:, q % GP]
                at = p * (2 * 128) + q // GP * 128
                c = by_group[:, at:at + 128] if isinstance(p, int) else by_group[:, bass.ds(at, 128)]
                mm = nc.tensor.matmul(ps6[:, q * F:(q + 1) * F], c, sel_n_sb[:], start=True, stop=True)
                if q == 2 * GP - 1:
                    mm.then_inc(aux6_full, 1)

            def x2_by_column(p, count):
                pe.wait_ge(x2_copied, p + 1)
                pe.wait_ge(aux6_free, count - 1)
                for g in range(GP):
                    c = x2_sb[:].rearrange("r (m g) -> r g m", g=GP)[:, g]
                    tp = nc.tensor.transpose(ps6[:, g * 128:(g + 1) * 128], c, eye_f_sb[:])
                tp.then_inc(aux6_full, 1)

            def outer_sums(p, count6, count7):
                pe.wait_ge(x2t_ready, p + 1)
                pe.wait_ge(bd_ready, p + 1)
                for g in range(GP):
                    if g == 0:
                        pe.wait_ge(aux7_free, count7 - 1)
                    if g == 2:
                        pe.wait_ge(aux6_free, count6 - 1)
                    bank = (ps7, ps6)[g // 2]
                    for s in range(2):
                        at = (g % 2 * 2 + s) * GC
                        for c in range(2):
                            mm = nc.tensor.matmul(bank[c * H:(c + 1) * H, at:at + GC], x2t[:, g, s * H:(s + 1) * H],
                                                  bd[:, s * GP + g, c].rearrange("p k b -> p (k b)"),
                                                  start=True, stop=True)
                    if g == 1:
                        mm.then_inc(aux7_full, 1)
                    if g == 3:
                        mm.then_inc(aux6_full, 1)

            def early(p, t, x, last=False):
                x0n = aux6(t, "X0n_" + x)
                x0_by_column(p - 1, 1, x0n)
                main2(p - 1, 1, 2)
                x0_by_column(p - 1, 2, x0n)
                if not last:
                    reps(p, 2)
                x0_by_column(p - 1, 3, x0n)
                main2(p - 1, 1, 3)
                x0_by_column(p - 1, 4, x0n)
                if not last:
                    main1(p, 0)
                x0_by_column(p - 1, 5, x0n)
                if not last:
                    main1(p, 1)
                x0_by_column(p - 1, 6, x0n)
                main2(p - 1, 2, 0)
                x0_by_column(p - 1, 7, x0n)
                for j in range(1, J2):
                    main2(p - 1, 2, j)
                if not last:
                    main1(p, 2)
                x2_by_column(p - 1, aux6(t, "X2T_" + x))
                main2(p, 0, 0)
                outer_sums(p - 1, aux6(t, "G1_" + x), aux7(t, "G0_" + x))

            def late(p, t, x, last=False):
                turn = x == "e" and not last
                main2(p, 0, 1)
                if turn:
                    transposes(t + 2, 0, aux7(t, "T0"))
                main2(p, 0, 2)
                if turn:
                    transposes(t + 2, 1, aux6(t, "T1"))
                main2(p, 0, 3)
                if turn:
                    main2(p, 1, 0)
                if not last:
                    left_factor(p + 2, 0, aux7(t, "A1_%s0" % x), t * 2 + 4)
                    left_factor(p + 2, 1, aux6(t, "A1_%s1" % x), t * 2 + 4)
                    reps(p + 1, 0)
                    reps(p + 1, 1)
                main2(p, 1, 1 if turn else 0)
                if not turn:
                    main2(p, 1, 1)
                x0_by_column(p, 0, aux6(t, "X0n_" + x))

            def mlp_in_a(q, first=0):
                end = PAIRS if first else PAIRS - 1
                nc.tensor.matmul(ring[:, q, first * 2 * HB:end * 2 * HB], wt1a_sb[:, q * 128:(q + 1) * 128],
                                 in_a[:, first:end].rearrange("p a s b -> p (a s b)"), start=(first == 0), stop=False)

            pe.wait_ge(consts_in, 16 * 3)
            transposes(1, 0, 1)
            transposes(1, 1, 1)
            left_factor(0, 0, 2, 2)
            left_factor(0, 1, 2, 2)
            for idx in range(L1_OPS):
                reps(-1, idx)
            pe.wait_ge(w0_ready, 1)
            for c in range(C1):
                main1(-1, c)
            left_factor(1, 0, 3, 2)
            left_factor(1, 1, 3, 2)
            for idx in range(L1_OPS):
                reps(0, idx)
            for c in range(C1):
                main1(0, c)
            pe.wait_ge(w_in, 16 * 12)
            main2(0, 0, 0)
            with pe.Fori(0, LAST) as t:
                late(t * 2, t, "e")
                early(t * 2 + 1, t, "e")
                late(t * 2 + 1, t, "o")
                early(t * 2 + 2, t, "o")
            p = PAIRS - 1
            late(p - 1, LAST, "e", last=True)
            early(p, LAST, "e", last=True)
            late(p, LAST, "o", last=True)
            x0_by_column(p, 1, aux6(LAST, "X0n_o"))
            for q, (i, j) in zip(range(2, 2 * GP, 2), ((1, 2), (1, 3), (2, 0))):
                main2(p, i, j)
                x0_by_column(p, q, aux6(LAST, "X0n_o"))
                x0_by_column(p, q + 1, aux6(LAST, "X0n_o"))
            for j in range(1, J2):
                main2(p, 2, j)
            pe.wait_ge(in_ready_v, 1)
            mlp_in_a(0)
            x2_by_column(p, aux6(LAST, "X2T_o"))
            mlp_in_a(1)
            outer_sums(p, aux6(LAST, "G1_o"), aux7(LAST, "G0_o"))
            mlp_in_a(2)
            mlp_in_a(3)

            pe.wait_ge(g_ready, 2 * PAIRS)
            for k in range(FH):
                for s, bank in enumerate((x1_ps, x2_ps)):
                    mm = nc.tensor.matmul(bank[s * H:(s + 1) * H, 0:PAIRS * HB], w2_sb[:, k],
                                          g_sb[:, s, k].rearrange("p a b -> p (a b)"),
                                          start=(k == 0), stop=(k == FH - 1))
            mm.then_inc(z3_done, 1)

            pe.wait_ge(in_ready_v, 2)
            for q in range(Q1):
                mlp_in_a(q, PAIRS - 1)
            pe.wait_ge(z3_ready_a, 1)
            pe.wait_ge(z3_ready_v, 1)
            for q in range(Q1):
                nc.tensor.matmul(ring[:, q], wt1b_sb[:, q * 128:(q + 1) * 128],
                                 in_b[:].rearrange("p a s b -> p (a s b)"), start=False, stop=True)\
                    .then_inc(h1_done, 1)
            for m, bank in enumerate((x1_ps, x2_ps)):
                for q in range(Q1):
                    if m == 0:
                        pe.wait_ge((h1_ready_a, h1_ready_v)[q % 2], q // 2 + 1)
                    mm = nc.tensor.matmul(bank[:], wt2_sb[:, q, m * 128:(m + 1) * 128], h1[:, q],
                                          start=(q == 0), stop=(q == Q1 - 1))
                mm.then_inc(h2_done, 1)
            pe.wait_ge(h2_ready_a, 1)
            for c, bank in enumerate((ps6, ps7)):
                nc.tensor.matmul(bank[c * H:c * H + 1, 0:B // 2], wt3_sb[:, 0:1], h2[:, 0, c * B // 2:(c + 1) * B // 2],
                                 start=True, stop=False)
            for c, bank in enumerate((ps6, ps7)):
                pe.wait_ge(h2_ready_v, c + 1)
                nc.tensor.matmul(bank[c * H:c * H + 1, 0:B // 2], wt3_sb[:, 1:2], h2[:, 1, c * B // 2:(c + 1) * B // 2],
                                 start=False, stop=True).then_inc(y_done, 1)

        @block.scalar
        def _(act):
            def copy(dst, src):
                return nc.scalar.activation(dst, src, ACT.Copy)

            def x0t_copy(t, part, count):
                bank, full, free = ((ps7, aux7_full, aux7_free), (ps6, aux6_full, aux6_free))[part]
                act.wait_ge(full, count)
                for dst, src in x0t_pieces(t, part, bank):
                    cp = copy(dst, src)
                cp.then_inc(free, 1)
                act.wait_ge(free, count)
                act.sem_inc(x0t_ready, 1)

            def a1_copy(parity, s, count):
                bank, full, free = ((ps7, aux7_full, aux7_free), (ps6, aux6_full, aux6_free))[s]
                act.wait_ge(full, count)
                copy(a1[:, parity, s], bank[:]).then_inc(free, 1)
                act.wait_ge(free, count)
                act.sem_inc(a1_ready, 1)

            def b_copy(p):
                act.wait_ge(x1_done, p + 1)
                if not (isinstance(p, int) and p == 0):
                    for s in range(2):
                        act.wait_ge(x1_stored[s], p * 16)
                copy(x1_sb[:], x1_ps[:]).then_inc(b_copied, 1)

            def bd_build(t, p, name):
                act.wait_ge(aux6_full, aux6(t, name))
                for b in range(GB):
                    cp = nc.scalar.activation(bd[:, :, :, 0:FH, b].rearrange("p q c k -> p (q c) k"),
                                              ps6[:, 0:2 * GP * F].rearrange("p (q k) -> p q k", k=FH),
                                              ACT.Copy, scale=mask_sb[:, b:b + 1])
                cp.then_inc(aux6_free, 1)
                act.wait_ge(aux6_free, aux6(t, name))
                act.sem_inc(bd_ready, 1)

            def x2_copy(p):
                act.wait_ge(l2_done, p * I2 + I2)
                copy(x2_sb[:], x2_ps[:]).then_inc(x2_copied, 1)

            def x2t_copy(t, name):
                act.wait_ge(aux6_full, aux6(t, name))
                copy(x2t[:].rearrange("p g c -> p (g c)"), ps6[:]).then_inc(aux6_free, 1)
                act.wait_ge(aux6_free, aux6(t, name))
                act.sem_inc(x2t_ready, 1)

            def g_copy(t, p, odd):
                x = "eo"[odd]
                for part, (bank, full, free, count) in enumerate((
                        (ps7, aux7_full, aux7_free, aux7(t, "G0_" + x)), (ps6, aux6_full, aux6_free, aux6(t, "G1_" + x)))):
                    act.wait_ge(full, count)
                    src = bank[:, 0:4 * GC].rearrange("p (g m b) -> p m b g", g=2, b=GB)
                    dst = g_sb[:].rearrange("p s k a (b g) -> p (s k) (a b) g", g=GP)
                    dst = dst[:, :, p * GB:(p + 1) * GB] if isinstance(p, int) else dst[:, :, bass.ds(p * GB, GB)]
                    dst = dst[:, :, :, 2 * part:2 * part + 2]
                    copy(dst, src).then_inc(free, 1)
                    act.wait_ge(free, count)
                    act.sem_inc(g_ready, 1)

            def early(p, t, odd, last=False):
                x2_copy(p - 1)
                x2t_copy(t, "X2T_" + "eo"[odd])
                if not last:
                    b_copy(p + 1)
                g_copy(t, p - 1, odd)

            def late(p, t, odd, last=False):
                x = "eo"[odd]
                if not last:
                    if not odd:
                        x0t_copy(t + 1, 0, aux7(t, "T0"))
                        x0t_copy(t + 1, 1, aux6(t, "T1"))
                    a1_copy(odd, 0, aux7(t, "A1_%s0" % x))
                    a1_copy(odd, 1, aux6(t, "A1_%s1" % x))
                bd_build(t, p, "X0n_" + x)

            x0t_copy(0, 0, 1)
            a1_copy(0, 0, 2)
            b_copy(0)
            a1_copy(1, 0, 3)
            b_copy(1)
            act.wait_ge(landed[1], 16 * F)
            act.wait_ge(x0t_ready, 2)
            e, left, hi, mid, lo = split_views(1, 0, F)
            copy(hi, e).then_inc(split_step, 1)
            act.wait_ge(split_step, 3 * 2 + 2)
            copy(mid, left).then_inc(split_step, 1)
            act.wait_ge(w_in, 16 * 12)
            act.wait_ge(sum_cols, 1)
            with act.Fori(0, LAST) as t:
                late(t * 2, t, 0)
                early(t * 2 + 1, t, 0)
                late(t * 2 + 1, t, 1)
                early(t * 2 + 2, t, 1)
            late(PAIRS - 2, LAST, 0, True)
            early(PAIRS - 1, LAST, 0, last=True)
            late(PAIRS - 1, LAST, 1, True)
            x2_copy(PAIRS - 1)
            x2t_copy(LAST, "X2T_o")
            g_copy(LAST, PAIRS - 1, 1)

            act.wait_ge(z3_done, 1)
            copy(in_b[0:H, :, 0, :], x1_ps[0:H, 0:PAIRS * HB].rearrange("p (a b) -> p a b", b=HB))\
                .then_inc(z3_ready_a, 1)
            for q in range(0, Q1, 2):
                act.wait_ge(h1_done, q + 1)
                nc.scalar.activation(h1[:, q], ring[:, q], ACT.Relu, bias=bt1_sb[:, q:q + 1])\
                    .then_inc(h1_ready_a, 1)
            act.wait_ge(h2_done, 1)
            nc.scalar.activation(h2[:, 0], x1_ps[:], ACT.Relu, bias=bt2_sb[:, 0:1]).then_inc(h2_ready_a, 1)


def _field_pairs():
    rows = []
    for c in range(C1):
        for p in range(128):
            k, f = c * KC + p // F, p % F
            ok = p < KC * F and (k < KD - 1 or (k == KD - 1 and f < F // 2))
            rows.append((f, (f + k) % F) if ok else None)
    return rows


def kernel(**inputs):
    import ml_dtypes
    import concourse.bacc as _bacc
    from concourse.bass_utils import run_bass_kernel_spmd as _run

    x = {k: np.asarray(v) for k, v in inputs.items()}
    bf = ml_dtypes.bfloat16
    w0 = x["L0_rec_W0"]
    w0a = np.zeros((C1 * 128, H), w0.dtype)
    w0b = np.zeros((C1 * 128, H), w0.dtype)
    sel_b1 = np.zeros((F, C1, 128), bf)
    for r, fh in enumerate(_field_pairs()):
        if fh is None:
            continue
        f, h = fh
        w0a[r] = w0[f * F + h]
        if f != h:
            w0b[r] = w0[h * F + f]
        sel_b1[h, r // 128, r % 128] = 1
    by_block = lambda w: np.ascontiguousarray(w.reshape(C1, 128, H).transpose(1, 0, 2))
    w1 = x["L0_rec_W1"].reshape(I2, U2, J2, V2, H).transpose(1, 3, 0, 2, 4).reshape(128, I2, J2, H)
    w2 = x["L0_rec_W2"].reshape(2, FH, H, H).transpose(0, 2, 1, 3).reshape(2 * H, FH, H)
    sel_a1 = np.zeros((F, 128), bf)
    for p in range(KC * F):
        sel_a1[p % F, p] = 1
    three = lambda a: np.concatenate([a] * PARTS, axis=0)
    mask = np.zeros((128, GB), np.float32)
    for p in range(128):
        mask[p, p % GB] = 1
    arrays = {
        "ids": x["ids"].reshape(TILES, 128, F).transpose(1, 0, 2),
        "dense_t": x["dense_ctx"].T,
        "w0a": by_block(w0a), "w0b": by_block(w0b), "w1": w1, "w2": w2,
        "wt1": x["W_top1"], "bt1": x["b_top1"].reshape(Q1, 128).T,
        "wt2": x["W_top2"].reshape(Q1, 128, M2).transpose(1, 0, 2), "bt2": x["b_top2"].reshape(Q2, 128).T,
        "wt3": x["W_top3"].reshape(Q2, 128).T,
        "sel_a1": three(sel_a1), "sel_b1": three(sel_b1),
        "sel_n": three(np.eye(F, dtype=bf)), "eye_f": np.eye(128, dtype=np.float32),
        "eye_b": np.eye(128, dtype=bf), "mask": mask,
    }
    for f in range(F):
        arrays[f"tbl_{f}"] = x[f"tbl_{f}"]
    arrays = {k: np.ascontiguousarray(v) for k, v in arrays.items()}

    nc = _bacc.Bacc("TRN2", target_bir_lowering=False, num_devices=1)
    aps = {k: nc.dram_tensor(k, v.shape, mybir.dt.from_np(v.dtype), kind="ExternalInput").ap()
           for k, v in arrays.items()}
    out = nc.dram_tensor("y", (B, 1), mybir.dt.float32, kind="ExternalOutput").ap()
    x0_rows = nc.dram_tensor("x0_rows", (PAIRS, F, 2, N), mybir.dt.float32).ap()
    x1_rows = nc.dram_tensor("x1_rows", (PAIRS, 2, V2, J2, N), mybir.dt.float32).ap()
    tables = [aps.pop(f"tbl_{f}") for f in range(F)]
    dlrm_tower(nc, tables=tables, x0_rows=x0_rows, x1_rows=x1_rows, out=out.rearrange("b o -> o b"), **aps)
    r = _run(nc, [arrays], core_ids=[0])
    return r.results[0]["y"]
```
